# Optimizing a Trainium2 kernel written in Bass

```python
import numpy as np
import jax
import jax.numpy as jnp

def _softmax(x, axis=-1):
    return jax.nn.softmax(x, axis=axis)

def _gelu(x):
    return jax.nn.gelu(x, approximate=True)

def _silu(x):
    return jax.nn.silu(x)

def _sigmoid(x):
    return jax.nn.sigmoid(x)

def _layernorm(x, axis=-1, eps=1e-05):
    m = jnp.mean(x, axis=axis, keepdims=True)
    v = jnp.var(x, axis=axis, keepdims=True)
    return (x - m) / jnp.sqrt(v + eps)

def _scatter_add(tgt, idx, src, axis=0):
    return tgt.at[idx].add(src)

def _segment_sum(src, seg, n):
    return jax.ops.segment_sum(src, seg, n)
kernel_name = 'mk_adaln_ffn_d1_seqx_r4_7d5846'

def setup_inputs(seed: int=0):
    np.random.seed(seed)
    _w = jnp.asarray

    def _rec_inputs():
        import jax
        import jax.numpy as jnp
        _rk = jax.random.key(seed)
        x = -0.000125 + 0.9999 * jax.random.normal(jax.random.fold_in(_rk, 1), (64, 64, 1024), jnp.float32)
        _lenS = 64 - jax.random.randint(jax.random.fold_in(_rk, 7), (64,), 0, max(1, 64 // 4) + 1, jnp.int32)
        _lenS2 = 64 - jax.random.randint(jax.random.fold_in(_rk, 8), (64,), 0, max(1, 64 // 4) + 1, jnp.int32)
        cond_128 = 0.0061147 + 1.02565 * jax.random.normal(jax.random.fold_in(_rk, 11), (64, 128), jnp.float32)
        return (x, cond_128)
    x, cond_128 = _rec_inputs()

    def _L0_cond_setup():
        import jax, jax.numpy as jnp
        import numpy as np
        K = 8
        T = 1.0
        D_EMBD = 128
        IN_C = 64
        OUT_C = 64
        BS = 32
        H = 1024
        HID = 128
        key = jax.random.key(seed)
        ks = jax.random.split(key, 10)
        s = lambda fan_in: 1.0 / np.sqrt(fan_in)
        return {'x': jax.random.normal(ks[0], (BS, IN_C, H), dtype=jnp.float32), 'embedding': jax.random.normal(ks[1], (BS, D_EMBD), dtype=jnp.float32), 'W0': jax.random.normal(ks[2], (D_EMBD, HID), dtype=jnp.float32) * s(D_EMBD), 'b0': jnp.zeros((HID,), dtype=jnp.float32), 'W1': jax.random.normal(ks[3], (HID, HID), dtype=jnp.float32) * s(HID), 'b1': jnp.zeros((HID,), dtype=jnp.float32), 'W2': jax.random.normal(ks[4], (HID, K), dtype=jnp.float32) * s(HID), 'b2': jnp.zeros((K,), dtype=jnp.float32), 'weight': jax.random.normal(ks[5], (K, OUT_C, IN_C, 1), dtype=jnp.float32) * s(IN_C), 'bias_k': jax.random.normal(ks[6], (K, OUT_C), dtype=jnp.float32) * 0.1}
    _L0_cond_all = _L0_cond_setup()
    _L0_cond_in = {k: v for k, v in _L0_cond_all.items() if k in ('W0', 'b0', 'W1', 'b1', 'W2', 'b2', 'weight', 'bias_k')}
    del _L0_cond_all

    def _L0_ffn_setup():
        import jax, jax.numpy as jnp
        import numpy as np
        LORA_RANK = 16
        LORA_ALPHA = 16
        LORA_SCALE = LORA_ALPHA / LORA_RANK
        key = jax.random.key(seed)
        k1, k2, k3, k4, k5 = jax.random.split(key, 5)
        B, S, D_IN, D_OUT, N_LORA, R = (8, 512, 1024, 1024, 3, LORA_RANK)
        std = 1.0 / np.sqrt(D_IN)
        x = jax.random.normal(k1, (B, S, D_IN), dtype=jnp.float32)
        weight = jax.random.truncated_normal(k2, -3.0, 3.0, (D_OUT, D_IN), dtype=jnp.float32) * std
        bias = jax.random.normal(k3, (D_OUT,), dtype=jnp.float32) * 0.01
        lora_A = jax.random.normal(k4, (N_LORA, R, D_IN), dtype=jnp.float32) * std
        lora_B = jax.random.normal(k5, (N_LORA, D_OUT, R), dtype=jnp.float32) * 0.02
        lora_start_indices = jnp.arange(4, dtype=jnp.int64) * 2
        return {'x': x, 'weight': weight, 'bias': bias, 'lora_A': lora_A, 'lora_B': lora_B, 'lora_start_indices': lora_start_indices}
    _L0_ffn_all = _L0_ffn_setup()
    _L0_ffn_in = {k: v for k, v in _L0_ffn_all.items() if k in ('weight', 'bias', 'lora_A', 'lora_B', 'lora_start_indices')}
    del _L0_ffn_all
    return {'x': x, 'cond_128': cond_128, 'L0_cond_W0': _L0_cond_in['W0'], 'L0_cond_b0': _L0_cond_in['b0'], 'L0_cond_W1': _L0_cond_in['W1'], 'L0_cond_b1': _L0_cond_in['b1'], 'L0_cond_W2': _L0_cond_in['W2'], 'L0_cond_b2': _L0_cond_in['b2'], 'L0_cond_weight': _L0_cond_in['weight'], 'L0_cond_bias_k': _L0_cond_in['bias_k'], 'L0_ffn_weight': _L0_ffn_in['weight'], 'L0_ffn_bias': _L0_ffn_in['bias'], 'L0_ffn_lora_A': _L0_ffn_in['lora_A'], 'L0_ffn_lora_B': _L0_ffn_in['lora_B'], 'L0_ffn_lora_start_indices': _L0_ffn_in['lora_start_indices']}

def reference(x, cond_128, L0_cond_W0, L0_cond_b0, L0_cond_W1, L0_cond_b1, L0_cond_W2, L0_cond_b2, L0_cond_weight, L0_cond_bias_k, L0_ffn_weight, L0_ffn_bias, L0_ffn_lora_A, L0_ffn_lora_B, L0_ffn_lora_start_indices):
    import jax
    import jax.numpy as jnp

    def _L0_cond_ref(x, embedding, W0, b0, W1, b1, W2, b2, weight, bias_k):
        import jax, jax.numpy as jnp
        import numpy as np
        K = 8
        T = 1.0
        D_EMBD = 128
        IN_C = 64
        OUT_C = 64
        BS = 32
        H = 1024
        HID = 128
        h = jax.nn.gelu(embedding @ W0 + b0, approximate=False)
        h = jax.nn.gelu(h @ W1 + b1, approximate=False)
        att = jax.nn.softmax((h @ W2 + b2) / T, axis=-1)
        agg_w = jnp.einsum('bk,koi->boi', att, weight[..., 0])
        agg_b = att @ bias_k
        out = jnp.einsum('boi,bih->boh', agg_w, x) + agg_b[:, :, None]
        return out

    def _L0_ffn_ref(x, weight, bias, lora_A, lora_B, lora_start_indices):
        import jax, jax.numpy as jnp
        import numpy as np
        LORA_RANK = 16
        LORA_ALPHA = 16
        LORA_SCALE = LORA_ALPHA / LORA_RANK
        y = jnp.einsum('bsd,od->bso', x, weight) + bias
        B = x.shape[0]
        seg = jnp.searchsorted(lora_start_indices, jnp.arange(B), side='right') - 1
        adapter_idx = jnp.clip(seg - 1, 0, lora_A.shape[0] - 1)
        A = lora_A[adapter_idx]
        Bw = lora_B[adapter_idx]
        lo = jnp.einsum('bsr,bor->bso', jnp.einsum('bsd,brd->bsr', x, A), Bw) * LORA_SCALE
        use_lora = (seg > 0)[:, None, None]
        return y + jnp.where(use_lora, lo, jnp.zeros((), dtype=y.dtype))
    x = x + _L0_ffn_ref(_L0_cond_ref(x, cond_128, L0_cond_W0, L0_cond_b0, L0_cond_W1, L0_cond_b1, L0_cond_W2, L0_cond_b2, L0_cond_weight, L0_cond_bias_k), L0_ffn_weight, L0_ffn_bias, L0_ffn_lora_A, L0_ffn_lora_B, L0_ffn_lora_start_indices)
    return x

_drawn_inputs = setup_inputs


def setup_inputs(seed=0):
    import zlib

    import numpy as np

    out = dict(_drawn_inputs(seed))
    spreads = {'L0_cond_b0': (0.0, 0.593), 'L0_cond_b1': (0.0, 0.343), 'L0_cond_b2': (0.0, 0.315)}
    factors = {'L0_ffn_bias': 6.031}
    for name, (base, spread) in spreads.items():
        noise = np.random.default_rng([zlib.crc32(name.encode()), seed]).standard_normal(out[name].shape)
        drawn = base * np.exp(spread * noise) if base else spread * noise
        out[name] = jnp.asarray(drawn.astype(out[name].dtype))
    for name, factor in factors.items():
        out[name] = (out[name] * factor).astype(out[name].dtype)
    return out
```

```python
from contextlib import ExitStack

import concourse.bass as bass
from concourse import mybir

BATCH = 64
CHAN = 64
HID = 1024
EMB = 128
NMIX = 8
NLORA = 3
RANK = 16
P = 128
NPAIR = P // CHAN
TILES = BATCH // NPAIR
KC = HID // P
HALF = 512
NH = HID // HALF
LR = NLORA * RANK
LOW = 64
SLOTS = 4
GROUP = 2
GROWS = GROUP * P
BANK_KC = HALF // P
NBANK = KC // BANK_KC
REP = P // NMIX
OG = CHAN // REP
T_CHUNK = 1


def adaln_ffn(nc, x, cond_t, w0, b0, w1, b1, w2, b2, mixw, bias_k, w_t, ffn_bias, lora_a_t, lora_b_t, starts, out):
    F32 = mybir.dt.float32
    F32R = mybir.dt.float32r
    I32 = mybir.dt.int32
    ALU = mybir.AluOpType
    ACT = mybir.ActivationFunctionType
    AX_X = mybir.AxisListType.X

    agg_b_dram = nc.dram_tensor("agg_b_scratch", [BATCH, CHAN], F32, kind="Internal").ap()

    ctx = ExitStack()
    with ctx:
        def sb(name, shape, dt=F32):
            return ctx.enter_context(nc.sbuf_tensor(name, shape, dt))

        def ps(name, shape):
            return ctx.enter_context(nc.psum_tensor(name, shape, F32))

        def sem(name):
            return ctx.enter_context(nc.semaphore(name))

        w_hi = sb("w_hi", [P, KC, HID], F32R)
        w_lo = sb("w_lo", [P, KC, HID], F32R)
        w_stage = sb("w_stage", [P, SLOTS, HID])
        x_tile = sb("x_tile", [P, SLOTS, HID])
        u_hi = sb("u_hi", [P, SLOTS // GROUP, KC, GROWS], F32R)
        u_lo = sb("u_lo", [P, SLOTS // GROUP, KC, GROWS], F32R)
        u_sum = sb("u_sum", [P, NBANK, BANK_KC, P])
        out_tile = sb("out_tile", [P, 2, HID])
        mix_blk = sb("mix_blk", [P, TILES, P])
        agg_b_all = sb("agg_b_all", [P, BATCH * CHAN])
        a_stage = sb("a_stage", [P, KC, LR])
        a_parts = sb("a_parts", [P, KC, P], F32R)
        b_stage = sb("b_stage", [P, HID])
        b_hi = sb("b_hi", [P, HID], F32R)
        b_lo = sb("b_lo", [P, HID], F32R)
        t_low_a = sb("t_low_a", [LR, GROWS])
        t_sum = sb("t_sum", [LR, GROWS])
        t_masked = sb("t_masked", [LR, GROWS])
        t_parts = sb("t_parts", [P, 2, GROWS], F32R)
        cond_sb = sb("cond_sb", [EMB, BATCH])
        w0_sb = sb("w0_sb", [EMB, P])
        w1_sb = sb("w1_sb", [P, P])
        w2_sb = sb("w2_sb", [P, NMIX])
        b0_sb = sb("b0_sb", [P, 1])
        b1_sb = sb("b1_sb", [P, 1])
        b2_sb = sb("b2_sb", [BATCH, NMIX])
        h1 = sb("h1", [P, BATCH])
        h2 = sb("h2", [P, BATCH])
        logits = sb("logits", [BATCH, NMIX])
        top = sb("top", [BATCH, 1])
        neg_top = sb("neg_top", [BATCH, 1])
        expd = sb("expd", [BATCH, NMIX])
        exp_sum = sb("exp_sum", [BATCH, 1])
        exp_inv = sb("exp_inv", [BATCH, 1])
        att_rep = sb("att_rep", [BATCH, REP, NMIX])
        att_t = sb("att_t", [P, BATCH])
        att_diag = sb("att_diag", [P, REP, BATCH])
        diag = sb("diag", [P, REP])
        ident = sb("ident", [BATCH, BATCH])
        mixw_sb = sb("mixw_sb", [P, OG, 2, CHAN])
        bias_k_sb = sb("bias_k_sb", [NMIX, CHAN])
        agg_b_sb = sb("agg_b_sb", [BATCH, CHAN])
        starts_i = sb("starts_i", [LR, 2], I32)
        starts_f = sb("starts_f", [LR, 2])
        batch_i = sb("batch_i", [LR, BATCH], I32)
        batch_f = sb("batch_f", [LR, BATCH])
        want = sb("want", [LR, 2])
        mask_a = sb("mask_a", [LR, BATCH])
        mask_b = sb("mask_b", [LR, BATCH])
        mask = sb("mask", [LR, BATCH])

        out_ps = [[ps(f"out_ps{i}{h}", [P, HALF]) for h in range(NH)] for i in range(2)]
        mix_ps = [ps(f"mix_ps{h}", [P, BANK_KC, P]) for h in range(NBANK)]
        t_ps = ps("t_ps", [P, GROWS])
        cond_ps = ps("cond_ps", [P, HALF])
        setup_ps = [out_ps[0][0], out_ps[0][1], out_ps[1][0], out_ps[1][1]]

        x_in = [sem(f"x_in{s}") for s in range(SLOTS)]
        w_in = [sem(f"w_in{s}") for s in range(SLOTS)]
        cond_in = sem("cond_in")
        w1_in = sem("w1_in")
        w2_in = sem("w2_in")
        mixw_in = sem("mixw_in")
        bias_k_in = sem("bias_k_in")
        starts_in = sem("starts_in")
        a_in = sem("a_in")
        b_in = sem("b_in")
        consts_made = sem("consts_made")
        consts_used = sem("consts_used")
        b_cleared = sem("b_cleared")
        h1_summed = sem("h1_summed")
        h1_ready = sem("h1_ready")
        h2_summed = sem("h2_summed")
        h2_ready = sem("h2_ready")
        logits_summed = sem("logits_summed")
        logits_ready = sem("logits_ready")
        top_ready = sem("top_ready")
        exp_ready = sem("exp_ready")
        soft = sem("soft")
        att_ready = sem("att_ready")
        att_t_summed = sem("att_t_summed")
        att_t_ready = sem("att_t_ready")
        diag_ready = sem("diag_ready")
        agg_b_summed = sem("agg_b_summed")
        agg_b_ready = sem("agg_b_ready")
        agg_b_out = sem("agg_b_out")
        agg_b_in = sem("agg_b_in")
        mixw_summed = sem("mixw_summed")
        mixw_used = sem("mixw_used")
        blk_cleared = sem("blk_cleared")
        blk_even = sem("blk_even")
        blk_odd = sem("blk_odd")
        starts_ready = sem("starts_ready")
        mask_parts = sem("mask_parts")
        mask_ready = sem("mask_ready")
        parts_cleared = sem("parts_cleared")
        w_hi_ready = sem("w_hi_ready")
        w_lo_ready = sem("w_lo_ready")
        a_hi_ready = sem("a_hi_ready")
        a_lo_ready = sem("a_lo_ready")
        b_hi_ready = sem("b_hi_ready")
        b_lo_ready = sem("b_lo_ready")
        mix_done = sem("mix_done")
        u_summed = sem("u_summed")
        u_hi_ready = sem("u_hi_ready")
        u_lo_ready = sem("u_lo_ready")
        t_done = sem("t_done")
        t_low_copied = sem("t_low_copied")
        t_summed = sem("t_summed")
        t_masked_ready = sem("t_masked_ready")
        t_hi_ready = sem("t_hi_ready")
        t_lo_ready = sem("t_lo_ready")
        tile_done = sem("tile_done")
        tile_added = sem("tile_added")
        stored = [sem(f"stored{i}") for i in range(2)]

        block = ctx.enter_context(nc.Block())

        def all_steps(engine, step):
            for s in range(SLOTS):
                step(s, s)
            with engine.Fori(1, TILES // SLOTS - 1) as turn:
                for s in range(SLOTS):
                    step(turn * SLOTS + s, s)
            for s in range(SLOTS):
                step(TILES - SLOTS + s, s)

        def is_first(j, count):
            return isinstance(j, int) and j < count

        def has_next(j):
            return not isinstance(j, int) or j + GROUP < TILES

        def uses_before(j, s, ring):
            return (j - s % ring) // ring if isinstance(j, int) else (j - s % ring) // ring

        @block.sync
        def _(sp):
            sp.dma_start(cond_sb[:], cond_t).then_inc(cond_in, 16)
            sp.dma_start(w0_sb[:], w0).then_inc(cond_in, 16)
            for s in range(GROUP):
                sp.dma_start(x_tile[:, s, :], x[s]).then_inc(x_in[s], 16)
            for c in range(KC):
                if c >= SLOTS:
                    sp.wait_ge(w_hi_ready, c - SLOTS + 1)
                    sp.wait_ge(w_lo_ready, c - SLOTS + 1)
                sp.dma_start(w_stage[:, c % SLOTS, :], w_t[c]).then_inc(w_in[c % SLOTS], 16)
            for s in range(GROUP, SLOTS):
                sp.dma_start(x_tile[:, s, :], x[s]).then_inc(x_in[s], 16)

            def step(j, s):
                sp.wait_ge(tile_added, j + 1)
                sp.dma_start(out[j], out_tile[:, s % 2, :]).then_inc(stored[s % 2], 16)
                if not isinstance(j, int) or j + SLOTS < TILES:
                    sp.dma_start(x_tile[:, s, :], x[j + SLOTS]).then_inc(x_in[s], 16)

            all_steps(sp, step)
            for i in range(2):
                sp.wait_ge(stored[i], 16 * TILES // 2)

        @block.gpsimd
        def _(pool):
            pool.memset(diag[:], 1.0).then_inc(consts_used, 1)
            pool.wait_ge(consts_used, 1)
            pool.affine_select(out=diag[:], in_=diag[:], compare_op=ALU.is_ge, fill=0.0, base=0,
                               pattern=[[-NMIX, REP]], channel_multiplier=1).then_inc(consts_used, 1)
            pool.wait_ge(consts_used, 2)
            pool.affine_select(out=diag[:], in_=diag[:], compare_op=ALU.is_ge, fill=0.0, base=NMIX - 1,
                               pattern=[[NMIX, REP]], channel_multiplier=-1).then_inc(consts_made, 1)
            pool.memset(ident[:], 0.0).then_inc(consts_used, 1)
            pool.wait_ge(consts_used, 3)
            pool.affine_select(out=ident[:], in_=ident[:], compare_op=ALU.not_equal, fill=1.0, base=0,
                               pattern=[[-1, BATCH]], channel_multiplier=1).then_inc(consts_made, 1)
            pool.dma_start(bias_k_sb[:], bias_k).then_inc(bias_k_in, 16)
            pool.memset(mix_blk[:], 0.0).then_inc(blk_cleared, 1)
            pool.wait_ge(blk_cleared, 1)
            pool.memset(a_parts[:].bitcast(F32), 0.0).then_inc(parts_cleared, 1)
            pool.wait_ge(parts_cleared, 1)
            pool.memset(t_parts[32:LOW, :, :].bitcast(F32), 1.0).then_inc(parts_cleared, 1)
            pool.wait_ge(parts_cleared, 2)
            pool.memset(t_parts[P - 32:P, :, :].bitcast(F32), 0.0).then_inc(parts_cleared, 1)
            pool.wait_ge(parts_cleared, 3)
            pool.iota(batch_i[:], [[1, BATCH]], 0, 0).then_inc(consts_made, 1)
            pool.memset(want[:], 1.0).then_inc(consts_used, 1)
            pool.wait_ge(consts_used, 4)
            pool.affine_select(out=want[:, 0:1], in_=want[:, 0:1], compare_op=ALU.is_ge, fill=0.0,
                               base=RANK - 1, pattern=[[0, 1]], channel_multiplier=-1).then_inc(consts_made, 1)
            pool.affine_select(out=want[:, 1:2], in_=want[:, 1:2], compare_op=ALU.is_ge, fill=0.0,
                               base=-RANK, pattern=[[0, 1]], channel_multiplier=1).then_inc(consts_used, 1)
            pool.wait_ge(consts_used, 5)
            pool.affine_select(out=want[:, 1:2], in_=want[:, 1:2], compare_op=ALU.is_ge, fill=0.0,
                               base=2 * RANK - 1, pattern=[[0, 1]], channel_multiplier=-1).then_inc(consts_made, 1)

        @block.scalar
        def _(act):
            act.dma_start(b0_sb[:], b0).then_inc(cond_in, 16)
            act.dma_start(w1_sb[:], w1).then_inc(w1_in, 16)
            act.dma_start(b1_sb[:], b1).then_inc(w1_in, 16)
            act.dma_start(w2_sb[:], w2).then_inc(w2_in, 16)
            act.dma_start(b2_sb[:], b2.to_broadcast([BATCH, NMIX])).then_inc(w2_in, 16)
            for half in range(2):
                act.dma_start(mixw_sb[:, :, half, :], mixw).then_inc(mixw_in, 16)
            act.dma_start(starts_i[:, 0:1], starts[2:3, :].to_broadcast([LR, 1])).then_inc(starts_in, 16)
            act.dma_start(starts_i[0:RANK, 1:2], starts[1:2, :].to_broadcast([RANK, 1])).then_inc(starts_in, 16)
            act.dma_start(starts_i[RANK:LR, 1:2], starts[3:4, :].to_broadcast([LR - RANK, 1])).then_inc(starts_in, 16)
            act.dma_start(a_stage[:], lora_a_t).then_inc(a_in, 16)
            act.wait_ge(b_cleared, 1)
            act.dma_start(b_stage[0:LR, :], lora_b_t).then_inc(b_in, 16)
            act.dma_start(b_stage[LR:LR + 1, :], ffn_bias).then_inc(b_in, 16)
            act.dma_start(b_stage[LOW:LOW + LR, :], lora_b_t).then_inc(b_in, 16)

            act.wait_ge(h1_summed, 1)
            act.activation(h1[:], cond_ps[:, 0:BATCH], ACT.Gelu, bias=b0_sb[:, 0:1]).then_inc(h1_ready, 1)
            act.wait_ge(h2_summed, 1)
            act.activation(h2[:], cond_ps[:, BATCH:2 * BATCH], ACT.Gelu, bias=b1_sb[:, 0:1]).then_inc(h2_ready, 1)
            act.wait_ge(top_ready, 1)
            act.activation(expd[:], logits[:], ACT.Exp, bias=neg_top[:, 0:1],
                           accum_out=exp_sum[:, 0:1]).then_inc(exp_ready, 1)
            act.wait_ge(agg_b_summed, 1)
            act.activation(agg_b_sb[:], cond_ps[0:BATCH, 256:256 + CHAN], ACT.Copy).then_inc(agg_b_ready, 1)
            act.wait_ge(agg_b_ready, 1)
            act.dma_start(agg_b_dram, agg_b_sb[:]).then_inc(agg_b_out, 16)
            act.wait_ge(agg_b_out, 16)
            act.dma_start(agg_b_all[:], agg_b_dram.rearrange("(a b) c -> a (b c)", a=1)
                          .to_broadcast([P, BATCH * CHAN])).then_inc(agg_b_in, 16)

            def w_high(c):
                act.wait_ge(w_in[c % SLOTS], 16 * (c // SLOTS + 1))
                act.activation(w_hi[:, c, :], w_stage[:, c % SLOTS, :], ACT.Copy).then_inc(w_hi_ready, 1)

            def blk_odd_part(n):
                act.wait_ge(mixw_summed, n + 1)
                q, h = n // 2, n % 2
                lo = CHAN + q * REP + h * REP // 2
                act.activation(mix_blk[CHAN:P, :, lo:lo + REP // 2].rearrange("p t o -> p o t"),
                               setup_ps[n % 4][CHAN:P, :].rearrange("p (o t b) -> p o t b", b=2, t=TILES)[:, :, :, 1],
                               ACT.Copy).then_inc(blk_odd, 1)

            act.wait_ge(blk_cleared, 1)
            for n in range(2 * OG):
                w_high(n)
                blk_odd_part(n)

            def u_high(j, s):
                for h in range(NBANK):
                    act.wait_ge(u_summed, NBANK * j + h + 1)
                    act.activation(u_hi[:, s // GROUP, h * BANK_KC:(h + 1) * BANK_KC, (s % GROUP) * P:(s % GROUP + 1) * P],
                                   u_sum[:, h, :, :], ACT.Copy).then_inc(u_hi_ready, 1)

            for j in range(GROUP):
                u_high(j, j)
            act.wait_ge(parts_cleared, 3)
            act.wait_ge(a_in, 16)
            act.activation(a_parts[:, :, 0:LR], a_stage[:], ACT.Copy).then_inc(a_hi_ready, 1)
            act.wait_ge(b_in, 48)
            act.activation(b_hi[:], b_stage[:], ACT.Copy).then_inc(b_hi_ready, 1)

            def step(j, s):
                if s % GROUP == 0:
                    g = j // GROUP if isinstance(j, int) else j // GROUP
                    act.wait_ge(t_done, g + 1)
                    act.activation(t_low_a[:], t_ps[LOW:LOW + LR, :], ACT.Copy).then_inc(t_low_copied, 1)
                    act.wait_ge(t_masked_ready, g + 1)
                    act.activation(t_parts[0:LR, s // GROUP, :], t_masked[:], ACT.Copy).then_inc(t_hi_ready, 1)
                if has_next(j):
                    u_high(j + GROUP, (s + GROUP) % SLOTS)

            all_steps(act, step)

        @block.vector
        def _(dve):
            dve.memset(b_stage[:], 0.0).then_inc(b_cleared, 1)

            def w_low(c):
                dve.wait_ge(w_hi_ready, c + 1)
                dve.tensor_tensor(w_lo[:, c, :], w_stage[:, c % SLOTS, :], w_hi[:, c, :].bitcast(F32),
                                  ALU.subtract).then_inc(w_lo_ready, 1)

            dve.wait_ge(logits_summed, 1)
            dve.wait_ge(w2_in, 32)
            dve.tensor_tensor(logits[:], cond_ps[0:BATCH, 128:128 + NMIX], b2_sb[:], ALU.add).then_inc(logits_ready, 1)
            dve.wait_ge(logits_ready, 1)
            dve.reduce_max(top[:], logits[:], AX_X).then_inc(soft, 1)
            dve.wait_ge(soft, 1)
            dve.tensor_scalar(neg_top[:], top[:], -1.0, None, ALU.mult).then_inc(top_ready, 1)
            dve.wait_ge(exp_ready, 1)
            dve.reciprocal(exp_inv[:], exp_sum[:]).then_inc(soft, 1)
            dve.wait_ge(soft, 2)
            dve.tensor_scalar(att_rep[:], expd[:].unsqueeze(1).to_broadcast([BATCH, REP, NMIX]),
                              exp_inv[:, 0:1], None, ALU.mult).then_inc(att_ready, 1)
            dve.wait_ge(att_t_summed, 1)
            dve.tensor_copy(att_t[:], cond_ps[:, 192:192 + BATCH]).then_inc(att_t_ready, 1)
            dve.wait_ge(consts_made, 5)
            dve.wait_ge(att_t_ready, 1)
            dve.tensor_tensor(att_diag[:], att_t[:].unsqueeze(1).to_broadcast([P, REP, BATCH]),
                              diag[:].unsqueeze(2).to_broadcast([P, REP, BATCH]), ALU.mult).then_inc(diag_ready, 1)
            w_low(0)

            dve.wait_ge(starts_in, 48)
            dve.tensor_copy(starts_f[:], starts_i[:]).then_inc(starts_ready, 1)
            dve.tensor_copy(batch_f[:], batch_i[:]).then_inc(starts_ready, 1)
            dve.wait_ge(starts_ready, 2)
            dve.tensor_scalar(mask_a[:], batch_f[:], starts_f[:, 0:1], want[:, 0:1], ALU.is_lt, ALU.is_equal).then_inc(mask_parts, 1)
            dve.tensor_scalar(mask_b[:], batch_f[:], starts_f[:, 1:2], want[:, 1:2], ALU.is_lt, ALU.is_equal).then_inc(mask_parts, 1)
            dve.wait_ge(mask_parts, 2)
            dve.tensor_tensor(mask[:], mask_a[:], mask_b[:], ALU.mult).then_inc(mask_ready, 1)

            dve.wait_ge(blk_cleared, 1)
            for n in range(2 * OG):
                dve.wait_ge(mixw_summed, n + 1)
                q, h = n // 2, n % 2
                lo = q * REP + h * REP // 2
                dve.tensor_copy(mix_blk[0:CHAN, :, lo:lo + REP // 2].rearrange("p t o -> p o t"),
                                setup_ps[n % 4][0:CHAN, :].rearrange("p (o t b) -> p o t b", b=2, t=TILES)[:, :, :, 0]).then_inc(blk_even, 1)
                if n in (1, 3, 5):
                    w_low(n // 2 + 1)

            def u_sums(j, s):
                for h in range(NBANK):
                    dve.wait_ge(mix_done, NBANK * j + h + 1)
                    if not is_first(j, 1):
                        dve.wait_ge(u_lo_ready, NBANK * (j - 1) + h + 1)
                    rows = agg_b_all[:, bass.ts(j, P)].unsqueeze(1).to_broadcast([P, BANK_KC, P])
                    dve.tensor_tensor(u_sum[:, h, :, :], mix_ps[h][:], rows, ALU.add).then_inc(u_summed, 1)

            def u_lows(j, s):
                for h in range(NBANK):
                    dve.wait_ge(u_hi_ready, NBANK * j + h + 1)
                    part = (slice(None), s // GROUP, slice(h * BANK_KC, (h + 1) * BANK_KC),
                            slice((s % GROUP) * P, (s % GROUP + 1) * P))
                    dve.tensor_tensor(u_lo[part], u_sum[:, h, :, :], u_hi[part].bitcast(F32),
                                      ALU.subtract).then_inc(u_lo_ready, 1)

            dve.wait_ge(agg_b_in, 16)
            for j in range(GROUP):
                u_sums(j, j)
                u_lows(j, j)
            for c in range(SLOTS, KC):
                w_low(c)
            dve.wait_ge(a_hi_ready, 1)
            dve.tensor_tensor(a_parts[:, :, LOW:LOW + LR], a_stage[:], a_parts[:, :, 0:LR].bitcast(F32),
                              ALU.subtract).then_inc(a_lo_ready, 1)
            dve.wait_ge(b_hi_ready, 1)
            dve.tensor_tensor(b_lo[:], b_stage[:], b_hi[:].bitcast(F32), ALU.subtract).then_inc(b_lo_ready, 1)

            def add_x(j, s):
                dve.wait_ge(tile_done, j + 1)
                if not is_first(j, 2):
                    dve.wait_ge(stored[s % 2], (j // 2) * 16 if isinstance(j, int) else (j - s % 2) * 8)
                for h in range(NH):
                    cols = slice(h * HALF, (h + 1) * HALF)
                    last = dve.tensor_tensor(out_tile[:, s % 2, cols], out_ps[s % 2][h][:], x_tile[:, s, cols], ALU.add)
                last.then_inc(tile_added, 1)

            def step(j, s):
                if not is_first(j, 1):
                    add_x(j - 1, (s - 1) % SLOTS)
                if s % GROUP == 0:
                    g = j // GROUP
                    dve.wait_ge(t_low_copied, g + 1)
                    if not is_first(j, 1):
                        dve.wait_ge(t_masked_ready, g)
                        dve.wait_ge(t_lo_ready, g)
                    dve.tensor_tensor(t_sum[:], t_ps[0:LR, :], t_low_a[:], ALU.add).then_inc(t_summed, 1)
                    dve.wait_ge(t_summed, g + 1)
                    own = mask[:, bass.ts(j // GROUP, GROUP * NPAIR)].unsqueeze(2).to_broadcast([LR, GROUP * NPAIR, CHAN])
                    dve.tensor_tensor(t_masked[:].rearrange("p (b c) -> p b c", c=CHAN),
                                      t_sum[:].rearrange("p (b c) -> p b c", c=CHAN), own,
                                      ALU.mult).then_inc(t_masked_ready, 1)
                    dve.wait_ge(t_hi_ready, g + 1)
                    dve.tensor_tensor(t_parts[LOW:LOW + LR, s // GROUP, :], t_masked[:],
                                      t_parts[0:LR, s // GROUP, :].bitcast(F32), ALU.subtract).then_inc(t_lo_ready, 1)
                if has_next(j):
                    u_sums(j + GROUP, (s + GROUP) % SLOTS)
                    u_lows(j + GROUP, (s + GROUP) % SLOTS)

            all_steps(dve, step)
            add_x(TILES - 1, SLOTS - 1)

        @block.tensor
        def _(pe):
            pe.wait_ge(cond_in, 48)
            pe.matmul(cond_ps[:, 0:BATCH], w0_sb[:], cond_sb[:], start=True, stop=True).then_inc(h1_summed, 1)
            pe.wait_ge(w1_in, 32)
            pe.wait_ge(h1_ready, 1)
            pe.matmul(cond_ps[:, BATCH:2 * BATCH], w1_sb[:], h1[:], start=True, stop=True).then_inc(h2_summed, 1)
            pe.wait_ge(w2_in, 32)
            pe.wait_ge(h2_ready, 1)
            pe.matmul(cond_ps[0:BATCH, 128:128 + NMIX], h2[:], w2_sb[:], start=True, stop=True).then_inc(logits_summed, 1)
            pe.wait_ge(consts_made, 2)
            pe.wait_ge(att_ready, 1)
            pe.matmul(cond_ps[:, 192:192 + BATCH], att_rep[:].rearrange("b g k -> b (g k)"), ident[:],
                      start=True, stop=True).then_inc(att_t_summed, 1)
            pe.wait_ge(att_t_ready, 1)
            pe.wait_ge(bias_k_in, 16)
            pe.matmul(cond_ps[0:BATCH, 256:256 + CHAN], att_t[0:NMIX, :], bias_k_sb[:],
                      start=True, stop=True).then_inc(agg_b_summed, 1)
            pe.wait_ge(mixw_in, 32)
            pe.wait_ge(diag_ready, 1)
            for n in range(2 * OG):
                if n >= 4:
                    pe.wait_ge(blk_even, n - 3)
                    pe.wait_ge(blk_odd, n - 3)
                q, h = n // 2, n % 2
                pe.matmul(setup_ps[n % 4][:], mixw_sb[:, q, :, :].rearrange("p a i -> p (a i)"),
                          att_diag[:, h * REP // 2:(h + 1) * REP // 2, :].rearrange("p g b -> p (g b)"),
                          start=True, stop=True).then_inc(mixw_summed, 1)

            def mix_chunk(j, s, c):
                h, k = c // BANK_KC, c % BANK_KC
                if k == 0:
                    if c == 0:
                        if isinstance(j, int):
                            pe.wait_ge(x_in[s], 16 * (j // SLOTS + 1))
                        else:
                            pe.wait_ge(x_in[s], (j - s + SLOTS) * (16 // SLOTS))
                    if not is_first(j, 1):
                        pe.wait_ge(u_summed, NBANK * (j - 1) + h + 1)
                mm = pe.matmul(mix_ps[h][:, k, :], x_tile[:, s, c * P:(c + 1) * P], mix_blk[:, j, :],
                               start=True, stop=True)
                if k == BANK_KC - 1:
                    mm.then_inc(mix_done, 1)

            pe.wait_ge(blk_even, 2 * OG)
            pe.wait_ge(blk_odd, 2 * OG)
            for j in range(GROUP):
                for c in range(KC):
                    mix_chunk(j, j, c)

            def main_chunk(s, c, first_tile):
                lhs = (slice(None), s // GROUP, c, slice((s % GROUP) * P, (s % GROUP + 1) * P))
                if first_tile:
                    pe.wait_ge(w_hi_ready, c + 1)
                    pe.wait_ge(w_lo_ready, c + 1)
                for u_part, w_part in ((u_hi, w_hi), (u_hi, w_lo), (u_lo, w_hi)):
                    for h in range(NH):
                        pe.matmul(out_ps[s % 2][h][:], u_part[lhs], w_part[:, c, h * HALF:(h + 1) * HALF],
                                  start=(c == 0 and u_part is u_hi and w_part is w_hi), stop=False)

            def lora_down(g, parity):
                if not isinstance(g, int) or g > 0:
                    pe.wait_ge(t_summed, g)
                else:
                    pe.wait_ge(a_hi_ready, 1)
                    pe.wait_ge(a_lo_ready, 1)
                pe.wait_ge(u_lo_ready, NBANK * GROUP * (g + 1))
                for c in range(KC):
                    for u_part in (u_hi, u_lo):
                        mm = pe.matmul(t_ps[:], a_parts[:, c, :], u_part[:, parity, c, :],
                                       start=(c == 0 and u_part is u_hi), stop=(c == KC - 1 and u_part is u_lo))
                mm.then_inc(t_done, 1)

            def lora_up(j, s, first_tile):
                if first_tile:
                    pe.wait_ge(b_hi_ready, 1)
                    pe.wait_ge(b_lo_ready, 1)
                if s % GROUP == 0:
                    pe.wait_ge(t_hi_ready, j // GROUP + 1)
                    pe.wait_ge(t_lo_ready, j // GROUP + 1)
                lhs = t_parts[:, s // GROUP, (s % GROUP) * P:(s % GROUP + 1) * P]
                for part in (b_hi, b_lo):
                    for h in range(NH):
                        mm = pe.matmul(out_ps[s % 2][h][:], lhs, part[:, h * HALF:(h + 1) * HALF],
                                       start=False, stop=part is b_lo)
                mm.then_inc(tile_done, 1)

            def step(j, s):
                first_tile = is_first(j, 1)
                pe.wait_ge(u_lo_ready, NBANK * (j + 1))
                if not is_first(j, 2):
                    pe.wait_ge(tile_added, j - 1)
                for c in range(KC):
                    main_chunk(s, c, first_tile)
                    if c == T_CHUNK and s % GROUP == 0:
                        lora_down(j // GROUP, s // GROUP)
                    if c < KC // 2 and has_next(j):
                        for m in range(2):
                            mix_chunk(j + GROUP, (s + GROUP) % SLOTS, 2 * c + m)
                lora_up(j, s, first_tile)

            all_steps(pe, step)


def kernel(**inputs):
    import numpy as np
    import concourse.bacc as bacc
    from concourse.bass_utils import run_bass_kernel_spmd

    def layout(a, shape, axes):
        return np.ascontiguousarray(np.transpose(np.reshape(a, shape), axes))

    i = {name: np.asarray(a) for name, a in inputs.items()}
    arrays = {
        "x": i["x"].reshape(TILES, P, HID),
        "cond_t": layout(i["cond_128"], (BATCH, EMB), (1, 0)),
        "w0": i["L0_cond_W0"],
        "b0": i["L0_cond_b0"].reshape(P, 1),
        "w1": i["L0_cond_W1"],
        "b1": i["L0_cond_b1"].reshape(P, 1),
        "w2": i["L0_cond_W2"],
        "b2": i["L0_cond_b2"].reshape(1, NMIX),
        "mixw": layout(i["L0_cond_weight"], (NMIX, OG, REP, CHAN), (2, 0, 1, 3)).reshape(P, OG, CHAN),
        "bias_k": i["L0_cond_bias_k"],
        "w_t": layout(i["L0_ffn_weight"], (HID, KC, P), (1, 2, 0)),
        "ffn_bias": i["L0_ffn_bias"].reshape(1, HID),
        "lora_a_t": layout(i["L0_ffn_lora_A"], (LR, KC, P), (2, 1, 0)),
        "lora_b_t": layout(i["L0_ffn_lora_B"], (NLORA, HID, RANK), (0, 2, 1)).reshape(LR, HID),
        "starts": i["L0_ffn_lora_start_indices"].reshape(NLORA + 1, 1),
    }
    arrays = {name: np.ascontiguousarray(a) for name, a in arrays.items()}
    nc = bacc.Bacc("TRN2", target_bir_lowering=False, num_devices=1)
    args = {name: nc.dram_tensor(f"in_{name}", a.shape, mybir.dt.from_np(a.dtype), kind="ExternalInput").ap()
            for name, a in arrays.items()}
    out = nc.dram_tensor("out", (TILES, P, HID), mybir.dt.float32, kind="ExternalOutput").ap()
    adaln_ffn(nc, out=out, **args)
    r = run_bass_kernel_spmd(nc, [{f"in_{name}": a for name, a in arrays.items()}], core_ids=[0])
    return r.results[0]["out"].reshape(BATCH, CHAN, HID)
```

```python
from contextlib import ExitStack

import concourse.bass as bass
from concourse import mybir

BATCH = 64
CHAN = 64
HID = 1024
EMB = 128
NMIX = 8
NLORA = 3
RANK = 16
P = 128
NPAIR = P // CHAN
TILES = BATCH // NPAIR
KC = HID // P
HALF = 512
NH = HID // HALF
LR = NLORA * RANK
LOW = 64
SLOTS = 4
GROUP = 2
GROWS = GROUP * P
BANK_KC = HALF // P
NBANK = KC // BANK_KC
REP = P // NMIX
OSET = REP // NPAIR
OG = CHAN // OSET
EARLY = 4
COND_PARTS = {"cond": BATCH, "w0": P, "w1": P, "w2": NMIX, "b0": 1, "b1": 1}
WARM = (20, 5, 5, 18, 9)
DOWN_CHUNK = 1
FIRST_DOWN_CHUNK = 5
COLS = [slice(h * HALF, (h + 1) * HALF) for h in range(NH)]


def adaln_ffn(nc, x, cond_pack, b2, mixw, bias_k, w_t, ffn_bias, lora_a_t, lora_b_t, starts, out):
    F32 = mybir.dt.float32
    F32R = mybir.dt.float32r
    I32 = mybir.dt.int32
    ALU = mybir.AluOpType
    ACT = mybir.ActivationFunctionType
    AX_X = mybir.AxisListType.X

    agg_b_dram = nc.dram_tensor("agg_b_scratch", [BATCH, CHAN], F32, kind="Internal").ap()

    ctx = ExitStack()
    with ctx:
        def sb(name, shape, dt=F32):
            return ctx.enter_context(nc.sbuf_tensor(name, shape, dt))

        def ps(name, shape):
            return ctx.enter_context(nc.psum_tensor(name, shape, F32))

        def sem(name):
            return ctx.enter_context(nc.semaphore(name))

        w_hi = sb("w_hi", [P, KC, HID], F32R)
        w_lo = sb("w_lo", [P, KC, HID], F32R)
        x_tile = sb("x_tile", [P, SLOTS, HID])
        u_hi = sb("u_hi", [P, SLOTS // GROUP, KC, GROWS], F32R)
        u_lo = sb("u_lo", [P, SLOTS // GROUP, KC, GROWS], F32R)
        u_sum = sb("u_sum", [P, NBANK, BANK_KC, P])
        out_tile = sb("out_tile", [P, 2, HID])
        w_ring = sb("w_ring", [P, SLOTS, HID])
        w_stage = [w_ring[:, n, :] for n in range(SLOTS)] + [out_tile[:, n, :] for n in range(2)]
        mix_blk = sb("mix_blk", [P, TILES, P])
        agg_b_all = sb("agg_b_all", [P, BATCH * CHAN])
        a_stage = sb("a_stage", [P, KC, LR])
        a_parts = sb("a_parts", [P, KC, P], F32R)
        b_stage = sb("b_stage", [P, HID])
        b_hi = sb("b_hi", [P, HID], F32R)
        b_lo = sb("b_lo", [P, HID], F32R)
        t_low_a = sb("t_low_a", [LR, GROWS])
        t_sum = sb("t_sum", [LR, GROWS])
        t_masked = sb("t_masked", [LR, GROWS])
        t_parts = sb("t_parts", [P, 2, GROWS], F32R)
        cond_all = sb("cond_all", [P, sum(COND_PARTS.values())])
        cond_part, at = {}, 0
        for name, width in COND_PARTS.items():
            cond_part[name] = cond_all[:, at:at + width]
            at += width
        warm = sb("warm", [P, 1])
        idle = sb("idle", [P, P], mybir.dt.bfloat16)
        b2_sb = sb("b2_sb", [BATCH, NMIX])
        h1 = sb("h1", [P, BATCH])
        h2 = sb("h2", [P, BATCH])
        logits = sb("logits", [BATCH, NMIX])
        top = sb("top", [BATCH, 1])
        neg_top = sb("neg_top", [BATCH, 1])
        expd = sb("expd", [BATCH, NMIX])
        exp_sum = sb("exp_sum", [BATCH, 1])
        exp_inv = sb("exp_inv", [BATCH, 1])
        att_rep = sb("att_rep", [BATCH, REP, NMIX])
        att_t = sb("att_t", [NMIX, BATCH])
        att_diag = sb("att_diag", [P, OSET, TILES])
        diag = sb("diag", [P, REP])
        ident = sb("ident", [BATCH, BATCH])
        mixw_sb = sb("mixw_sb", [P, OG, NPAIR, CHAN])
        bias_k_sb = sb("bias_k_sb", [NMIX, CHAN])
        agg_b_sb = sb("agg_b_sb", [BATCH, CHAN])
        starts_i = sb("starts_i", [LR, 2], I32)
        starts_f = sb("starts_f", [LR, 2])
        batch_i = sb("batch_i", [LR, BATCH], I32)
        batch_f = sb("batch_f", [LR, BATCH])
        want = sb("want", [LR, 2])
        mask_a = sb("mask_a", [LR, BATCH])
        mask_b = sb("mask_b", [LR, BATCH])
        mask = sb("mask", [LR, BATCH])

        out_ps = [[ps(f"out_ps{i}{h}", [P, HALF]) for h in range(NH)] for i in range(2)]
        mix_ps = [ps(f"mix_ps{h}", [P, BANK_KC, P]) for h in range(NBANK)]
        t_ps = ps("t_ps", [P, GROWS])
        cond_ps = ps("cond_ps", [P, HALF])
        setup_ps = [out_ps[0][0], out_ps[0][1], out_ps[1][0], out_ps[1][1]]

        x_in = [sem(f"x_in{s}") for s in range(SLOTS)]
        w_in = [sem(f"w_in{c}") for c in range(KC)]
        cond_in = sem("cond_in")
        b2_in = sem("b2_in")
        warm_ready = sem("warm_ready")
        warmed = sem("warmed")
        idle_ready = sem("idle_ready")
        mixw_cleared = sem("mixw_cleared")
        mixw_in = sem("mixw_in")
        bias_k_in = sem("bias_k_in")
        starts_in = sem("starts_in")
        a_in = sem("a_in")
        b_in = sem("b_in")
        consts_begun = sem("consts_begun")
        diag_made = sem("diag_made")
        ident_made = sem("ident_made")
        want_made = sem("want_made")
        b_cleared = sem("b_cleared")
        h1_summed = sem("h1_summed")
        h1_ready = sem("h1_ready")
        h2_summed = sem("h2_summed")
        h2_ready = sem("h2_ready")
        logits_summed = sem("logits_summed")
        logits_ready = sem("logits_ready")
        top_ready = sem("top_ready")
        exp_ready = sem("exp_ready")
        soft = sem("soft")
        att_ready = sem("att_ready")
        att_t_summed = sem("att_t_summed")
        att_t_ready = sem("att_t_ready")
        diag_ready = sem("diag_ready")
        agg_b_summed = sem("agg_b_summed")
        agg_b_ready = sem("agg_b_ready")
        agg_b_early = sem("agg_b_early")
        agg_b_early_ready = sem("agg_b_early_ready")
        agg_b_out = sem("agg_b_out")
        agg_b_in = sem("agg_b_in")
        mixw_summed = sem("mixw_summed")
        blk_cleared = sem("blk_cleared")
        blk_even = sem("blk_even")
        blk_odd = sem("blk_odd")
        starts_ready = sem("starts_ready")
        mask_parts = sem("mask_parts")
        mask_ready = sem("mask_ready")
        parts_cleared = sem("parts_cleared")
        w_hi_ready = sem("w_hi_ready")
        w_lo_ready = sem("w_lo_ready")
        a_hi_ready = sem("a_hi_ready")
        a_lo_ready = sem("a_lo_ready")
        b_hi_ready = sem("b_hi_ready")
        b_lo_ready = sem("b_lo_ready")
        mix_done = sem("mix_done")
        u_summed = sem("u_summed")
        u_hi_ready = sem("u_hi_ready")
        u_lo_ready = sem("u_lo_ready")
        t_done = sem("t_done")
        t_low_copied = sem("t_low_copied")
        t_summed = sem("t_summed")
        t_masked_ready = sem("t_masked_ready")
        t_hi_ready = sem("t_hi_ready")
        t_lo_ready = sem("t_lo_ready")
        tile_done = sem("tile_done")
        tile_added = sem("tile_added")
        stored = [sem(f"stored{i}") for i in range(2)]

        block = ctx.enter_context(nc.Block())

        def all_steps(engine, step):
            for s in range(SLOTS):
                step(s, s)
            with engine.Fori(1, TILES // SLOTS - 1) as turn:
                for s in range(SLOTS):
                    step(turn * SLOTS + s, s)
            for s in range(SLOTS):
                step(TILES - SLOTS + s, s)

        def is_first(j, count):
            return isinstance(j, int) and j < count

        def is_last(j):
            return isinstance(j, int) and j == TILES - 1

        def has_next(j):
            return not isinstance(j, int) or j + GROUP < TILES

        @block.sync
        def _(sp):
            sp.dma_start(cond_all[:], cond_pack).then_inc(cond_in, 16)
            sp.dma_start(b2_sb[:], b2.to_broadcast([BATCH, NMIX])).then_inc(b2_in, 16)
            sp.dma_start(bias_k_sb[:], bias_k).then_inc(bias_k_in, 16)
            sp.wait_ge(mixw_cleared, 1)
            for b in range(NPAIR):
                sp.dma_start(mixw_sb[b * CHAN:(b + 1) * CHAN, :, b, :], mixw).then_inc(mixw_in, 16)

            def load_w(c):
                if c >= len(w_stage):
                    sp.wait_ge(w_hi_ready, c - len(w_stage) + 1)
                    sp.wait_ge(w_lo_ready, c - len(w_stage) + 1)
                sp.dma_start(w_stage[c % len(w_stage)], w_t[c]).then_inc(w_in[c], 16)

            for s in range(GROUP):
                load_w(s)
                sp.dma_start(x_tile[:, s, :], x[s]).then_inc(x_in[s], 16)
            for c in range(GROUP, len(w_stage) - 1):
                load_w(c)
            sp.dma_start(x_tile[:, 2, :], x[2]).then_inc(x_in[2], 16)
            sp.wait_ge(agg_b_ready, 1)
            sp.dma_start(agg_b_dram, agg_b_sb[:]).then_inc(agg_b_out, 16)
            for c in range(len(w_stage) - 1, KC):
                load_w(c)
            sp.dma_start(x_tile[:, 3, :], x[3]).then_inc(x_in[3], 16)
            sp.wait_ge(agg_b_out, 16)
            sp.dma_start(agg_b_all[:, EARLY * CHAN:BATCH * CHAN],
                         agg_b_dram[EARLY:BATCH, :].rearrange("(a b) c -> a (b c)", a=1)
                         .to_broadcast([P, (BATCH - EARLY) * CHAN])).then_inc(agg_b_in, 16)

            def step(j, s):
                if is_last(j):
                    for h in range(NH):
                        sp.wait_ge(tile_added, j + h + 1)
                        sp.dma_start(out[j][:, COLS[h]], out_tile[:, s % 2, COLS[h]]).then_inc(stored[s % 2], 16)
                    return
                sp.wait_ge(tile_added, j + 1)
                sp.dma_start(out[j], out_tile[:, s % 2, :]).then_inc(stored[s % 2], 16)
                if not isinstance(j, int) or j + SLOTS < TILES:
                    sp.dma_start(x_tile[:, s, :], x[j + SLOTS]).then_inc(x_in[s], 16)

            all_steps(sp, step)
            sp.wait_ge(stored[0], 16 * TILES // 2)
            sp.wait_ge(stored[1], 16 * (TILES // 2 - 1 + NH))

        @block.gpsimd
        def _(pool):
            pool.memset(mixw_sb[:], 0.0).then_inc(mixw_cleared, 1)
            pool.wait_ge(mixw_cleared, 1)
            pool.memset(diag[:], 1.0).then_inc(consts_begun, 1)
            pool.wait_ge(consts_begun, 1)
            pool.affine_select(out=diag[:], in_=diag[:], compare_op=ALU.is_ge, fill=0.0, base=0,
                               pattern=[[-NMIX, REP]], channel_multiplier=1).then_inc(consts_begun, 1)
            pool.wait_ge(consts_begun, 2)
            pool.affine_select(out=diag[:], in_=diag[:], compare_op=ALU.is_ge, fill=0.0, base=NMIX - 1,
                               pattern=[[NMIX, REP]], channel_multiplier=-1).then_inc(diag_made, 1)
            pool.memset(ident[:], 0.0).then_inc(consts_begun, 1)
            pool.wait_ge(consts_begun, 3)
            pool.affine_select(out=ident[:], in_=ident[:], compare_op=ALU.not_equal, fill=1.0, base=0,
                               pattern=[[-1, BATCH]], channel_multiplier=1).then_inc(ident_made, 1)
            pool.memset(b_stage[:], 0.0).then_inc(b_cleared, 1)
            pool.dma_start(starts_i[:, 0:1], starts[2:3, :].to_broadcast([LR, 1])).then_inc(starts_in, 16)
            pool.dma_start(starts_i[0:RANK, 1:2], starts[1:2, :].to_broadcast([RANK, 1])).then_inc(starts_in, 16)
            pool.dma_start(starts_i[RANK:LR, 1:2], starts[3:4, :].to_broadcast([LR - RANK, 1])).then_inc(starts_in, 16)
            pool.dma_start(a_stage[:], lora_a_t).then_inc(a_in, 16)
            pool.wait_ge(b_cleared, 1)
            pool.dma_start(b_stage[0:LR, :], lora_b_t).then_inc(b_in, 16)
            pool.dma_start(b_stage[LR:LR + 1, :], ffn_bias).then_inc(b_in, 16)
            pool.dma_start(b_stage[LOW:LOW + LR, :], lora_b_t).then_inc(b_in, 16)
            pool.memset(a_parts[:].bitcast(F32), 0.0).then_inc(parts_cleared, 1)
            pool.wait_ge(parts_cleared, 1)
            pool.memset(t_parts[32:LOW, :, :].bitcast(F32), 1.0).then_inc(parts_cleared, 1)
            pool.wait_ge(parts_cleared, 2)
            pool.memset(t_parts[P - 32:P, :, :].bitcast(F32), 0.0).then_inc(parts_cleared, 1)
            pool.wait_ge(parts_cleared, 3)
            pool.iota(batch_i[:], [[1, BATCH]], 0, 0).then_inc(want_made, 1)
            pool.memset(want[:], 1.0).then_inc(consts_begun, 1)
            pool.wait_ge(consts_begun, 4)
            pool.affine_select(out=want[:, 0:1], in_=want[:, 0:1], compare_op=ALU.is_ge, fill=0.0,
                               base=RANK - 1, pattern=[[0, 1]], channel_multiplier=-1).then_inc(want_made, 1)
            pool.affine_select(out=want[:, 1:2], in_=want[:, 1:2], compare_op=ALU.is_ge, fill=0.0,
                               base=-RANK, pattern=[[0, 1]], channel_multiplier=1).then_inc(consts_begun, 1)
            pool.wait_ge(consts_begun, 5)
            pool.affine_select(out=want[:, 1:2], in_=want[:, 1:2], compare_op=ALU.is_ge, fill=0.0,
                               base=2 * RANK - 1, pattern=[[0, 1]], channel_multiplier=-1).then_inc(want_made, 1)

        @block.scalar
        def _(act):
            def w_high(c):
                act.wait_ge(w_in[c], 16)
                act.activation(w_hi[:, c, :], w_stage[c % len(w_stage)], ACT.Copy).then_inc(w_hi_ready, 1)

            act.wait_ge(warm_ready, 1)
            act.activation(warm[:, 0:1], warm[:, 0:1], ACT.Gelu).then_inc(warmed, 1)
            act.wait_ge(h1_summed, 1)
            act.activation(h1[:], cond_ps[:, 0:BATCH], ACT.Gelu, bias=cond_part["b0"]).then_inc(h1_ready, 1)
            act.wait_ge(h2_summed, 1)
            act.activation(h2[:], cond_ps[:, BATCH:2 * BATCH], ACT.Gelu, bias=cond_part["b1"]).then_inc(h2_ready, 1)
            act.wait_ge(warmed, 1)
            act.activation(warm[:, 0:1], warm[:, 0:1], ACT.Exp).then_inc(warmed, 1)
            act.wait_ge(top_ready, 1)
            act.activation(expd[:], logits[:], ACT.Exp, bias=neg_top[:, 0:1],
                           accum_out=exp_sum[:, 0:1]).then_inc(exp_ready, 1)
            w_high(0)
            act.wait_ge(diag_ready, 1)
            act.activation(att_t[:], cond_ps[0:NMIX, 192:192 + BATCH], ACT.Copy).then_inc(att_t_ready, 1)
            act.wait_ge(agg_b_summed, 1)
            act.activation(agg_b_sb[:], cond_ps[0:BATCH, 0:CHAN], ACT.Copy).then_inc(agg_b_ready, 1)

            def blk_odd_part(n):
                act.wait_ge(mixw_summed, n + 1)
                lo = CHAN + n * 2 * OSET
                act.activation(mix_blk[CHAN:P, :, lo:lo + 2 * OSET].rearrange("p t o -> p o t"),
                               setup_ps[n][CHAN:P, :].rearrange("p (o t) -> p o t", t=TILES),
                               ACT.Copy).then_inc(blk_odd, 1)

            act.wait_ge(blk_cleared, 2)
            for n in range(OG // 2):
                blk_odd_part(n)
                if n == 1:
                    w_high(1)
            act.wait_ge(agg_b_early, 1)
            act.activation(agg_b_all[:, 0:EARLY * CHAN], cond_ps[:, 256:256 + EARLY * CHAN], ACT.Copy).then_inc(agg_b_early_ready, 1)

            def u_high(j, s):
                for h in range(NBANK):
                    act.wait_ge(u_summed, NBANK * j + h + 1)
                    act.activation(u_hi[:, s // GROUP, h * BANK_KC:(h + 1) * BANK_KC, (s % GROUP) * P:(s % GROUP + 1) * P],
                                   u_sum[:, h, :, :], ACT.Copy).then_inc(u_hi_ready, 1)

            w_high(2)
            u_high(0, 0)
            w_high(3)
            w_high(4)
            u_high(1, 1)
            w_high(5)
            act.wait_ge(parts_cleared, 3)
            act.wait_ge(a_in, 16)
            act.activation(a_parts[:, :, 0:LR], a_stage[:], ACT.Copy).then_inc(a_hi_ready, 1)
            w_high(6)
            w_high(7)
            act.wait_ge(b_in, 48)
            act.activation(b_hi[:], b_stage[:], ACT.Copy).then_inc(b_hi_ready, 1)

            def step(j, s):
                if s % GROUP == 0:
                    g = j // GROUP
                    act.wait_ge(t_done, g + 1)
                    act.activation(t_low_a[:], t_ps[LOW:LOW + LR, :], ACT.Copy).then_inc(t_low_copied, 1)
                    act.wait_ge(t_masked_ready, g + 1)
                    act.activation(t_parts[0:LR, s // GROUP, :], t_masked[:], ACT.Copy).then_inc(t_hi_ready, 1)
                if has_next(j):
                    u_high(j + GROUP, (s + GROUP) % SLOTS)

            all_steps(act, step)

        @block.vector
        def _(dve):
            dve.memset(idle[:], 0.0).then_inc(idle_ready, 1)
            dve.memset(warm[:], 0.0).then_inc(warm_ready, 1)
            dve.memset(mix_blk[0:CHAN, :, CHAN:P], 0.0).then_inc(blk_cleared, 1)
            dve.memset(mix_blk[CHAN:P, :, 0:CHAN], 0.0).then_inc(blk_cleared, 1)

            def w_low(c):
                dve.wait_ge(w_hi_ready, c + 1)
                dve.tensor_tensor(w_lo[:, c, :], w_stage[c % len(w_stage)], w_hi[:, c, :].bitcast(F32),
                                  ALU.subtract).then_inc(w_lo_ready, 1)

            dve.wait_ge(logits_summed, 1)
            dve.wait_ge(b2_in, 16)
            dve.tensor_tensor(logits[:], cond_ps[0:BATCH, 128:128 + NMIX], b2_sb[:], ALU.add).then_inc(logits_ready, 1)
            dve.wait_ge(logits_ready, 1)
            dve.reduce_max(top[:], logits[:], AX_X).then_inc(soft, 1)
            dve.wait_ge(soft, 1)
            dve.tensor_scalar(neg_top[:], top[:], -1.0, None, ALU.mult).then_inc(top_ready, 1)
            dve.wait_ge(exp_ready, 1)
            dve.reciprocal(exp_inv[:], exp_sum[:]).then_inc(soft, 1)
            dve.wait_ge(soft, 2)
            dve.tensor_scalar(att_rep[:], expd[:].unsqueeze(1).to_broadcast([BATCH, REP, NMIX]),
                              exp_inv[:, 0:1], None, ALU.mult).then_inc(att_ready, 1)
            dve.wait_ge(att_t_summed, 1)
            dve.wait_ge(diag_made, 1)
            for b in range(NPAIR):
                rows, groups = slice(b * CHAN, (b + 1) * CHAN), slice(b * OSET, (b + 1) * OSET)
                own = cond_ps[rows, 192:192 + BATCH].rearrange("p (t b) -> p b t", b=NPAIR)[:, b, :]
                dve.tensor_tensor(att_diag[rows, :, :], own.unsqueeze(1).to_broadcast([CHAN, OSET, TILES]),
                                  diag[rows, groups].unsqueeze(2).to_broadcast([CHAN, OSET, TILES]),
                                  ALU.mult).then_inc(diag_ready, 1)
            w_low(0)

            for n in range(OG // 2):
                dve.wait_ge(mixw_summed, n + 1)
                lo = n * 2 * OSET
                dve.tensor_copy(mix_blk[0:CHAN, :, lo:lo + 2 * OSET].rearrange("p t o -> p o t"),
                                setup_ps[n][0:CHAN, :].rearrange("p (o t) -> p o t", t=TILES)).then_inc(blk_even, 1)
            w_low(1)

            def u_sums(j, s):
                for h in range(NBANK):
                    dve.wait_ge(mix_done, NBANK * j + h + 1)
                    if not is_first(j, 1):
                        dve.wait_ge(u_lo_ready, NBANK * (j - 1) + h + 1)
                    rows = agg_b_all[:, bass.ts(j, P)].unsqueeze(1).to_broadcast([P, BANK_KC, P])
                    dve.tensor_tensor(u_sum[:, h, :, :], mix_ps[h][:], rows, ALU.add).then_inc(u_summed, 1)

            def u_lows(j, s):
                for h in range(NBANK):
                    dve.wait_ge(u_hi_ready, NBANK * j + h + 1)
                    part = (slice(None), s // GROUP, slice(h * BANK_KC, (h + 1) * BANK_KC),
                            slice((s % GROUP) * P, (s % GROUP + 1) * P))
                    dve.tensor_tensor(u_lo[part], u_sum[:, h, :, :], u_hi[part].bitcast(F32),
                                      ALU.subtract).then_inc(u_lo_ready, 1)

            dve.wait_ge(agg_b_early_ready, 1)
            u_sums(0, 0)
            u_lows(0, 0)
            w_low(2)
            w_low(3)
            u_sums(1, 1)
            w_low(4)
            u_lows(1, 1)
            w_low(5)
            dve.wait_ge(a_hi_ready, 1)
            dve.tensor_tensor(a_parts[:, :, LOW:LOW + LR], a_stage[:], a_parts[:, :, 0:LR].bitcast(F32),
                              ALU.subtract).then_inc(a_lo_ready, 1)
            w_low(6)
            w_low(7)
            dve.wait_ge(want_made, 3)
            dve.wait_ge(starts_in, 48)
            dve.tensor_copy(starts_f[:], starts_i[:]).then_inc(starts_ready, 1)
            dve.tensor_copy(batch_f[:], batch_i[:]).then_inc(starts_ready, 1)
            dve.wait_ge(starts_ready, 2)
            dve.tensor_scalar(mask_a[:], batch_f[:], starts_f[:, 0:1], want[:, 0:1], ALU.is_lt, ALU.is_equal).then_inc(mask_parts, 1)
            dve.tensor_scalar(mask_b[:], batch_f[:], starts_f[:, 1:2], want[:, 1:2], ALU.is_lt, ALU.is_equal).then_inc(mask_parts, 1)
            dve.wait_ge(mask_parts, 2)
            dve.tensor_tensor(mask[:], mask_a[:], mask_b[:], ALU.mult).then_inc(mask_ready, 1)

            dve.wait_ge(b_hi_ready, 1)
            dve.tensor_tensor(b_lo[:], b_stage[:], b_hi[:].bitcast(F32), ALU.subtract).then_inc(b_lo_ready, 1)

            def add_x(j, s):
                dve.wait_ge(tile_done, j + 1)
                if is_first(j, 1):
                    dve.wait_ge(w_lo_ready, KC)
                if not is_first(j, 2):
                    dve.wait_ge(stored[s % 2], (j // 2) * 16 if isinstance(j, int) else (j - s % 2) * 8)
                for h in range(NH):
                    if is_last(j) and h > 0:
                        dve.wait_ge(tile_done, j + h + 1)
                    last = dve.tensor_tensor(out_tile[:, s % 2, COLS[h]], out_ps[s % 2][h][:], x_tile[:, s, COLS[h]], ALU.add)
                    if is_last(j) or h == NH - 1:
                        last.then_inc(tile_added, 1)

            def step(j, s):
                if not is_first(j, 1):
                    add_x(j - 1, (s - 1) % SLOTS)
                if s % GROUP == 0:
                    g = j // GROUP
                    dve.wait_ge(t_low_copied, g + 1)
                    if not is_first(j, 1):
                        dve.wait_ge(t_masked_ready, g)
                        dve.wait_ge(t_lo_ready, g)
                    dve.tensor_tensor(t_sum[:], t_ps[0:LR, :], t_low_a[:], ALU.add).then_inc(t_summed, 1)
                    dve.wait_ge(t_summed, g + 1)
                    own = mask[:, bass.ts(j // GROUP, GROUP * NPAIR)].unsqueeze(2).to_broadcast([LR, GROUP * NPAIR, CHAN])
                    dve.tensor_tensor(t_masked[:].rearrange("p (b c) -> p b c", c=CHAN),
                                      t_sum[:].rearrange("p (b c) -> p b c", c=CHAN), own,
                                      ALU.mult).then_inc(t_masked_ready, 1)
                    dve.wait_ge(t_hi_ready, g + 1)
                    dve.tensor_tensor(t_parts[LOW:LOW + LR, s // GROUP, :], t_masked[:],
                                      t_parts[0:LR, s // GROUP, :].bitcast(F32), ALU.subtract).then_inc(t_lo_ready, 1)
                if has_next(j):
                    if is_first(j, 1):
                        dve.wait_ge(agg_b_in, 16)
                    u_sums(j + GROUP, (s + GROUP) % SLOTS)
                    u_lows(j + GROUP, (s + GROUP) % SLOTS)

            all_steps(dve, step)
            add_x(TILES - 1, SLOTS - 1)

        @block.tensor
        def _(pe):
            def keep_warm(n):
                for _ in range(n):
                    pe.matmul(setup_ps[-1][:, 0:P], idle[:], idle[:], start=True, stop=True)

            pe.wait_ge(idle_ready, 1)
            keep_warm(WARM[0])
            pe.wait_ge(cond_in, 16)
            pe.matmul(cond_ps[:, 0:BATCH], cond_part["w0"], cond_part["cond"], start=True, stop=True).then_inc(h1_summed, 1)
            keep_warm(WARM[1])
            pe.wait_ge(h1_ready, 1)
            pe.matmul(cond_ps[:, BATCH:2 * BATCH], cond_part["w1"], h1[:], start=True, stop=True).then_inc(h2_summed, 1)
            keep_warm(WARM[2])
            pe.wait_ge(h2_ready, 1)
            pe.matmul(cond_ps[0:BATCH, 128:128 + NMIX], h2[:], cond_part["w2"], start=True, stop=True).then_inc(logits_summed, 1)
            keep_warm(WARM[3])
            pe.wait_ge(ident_made, 1)
            pe.wait_ge(att_ready, 1)
            pe.matmul(cond_ps[:, 192:192 + BATCH], att_rep[:].rearrange("b g k -> b (g k)"), ident[:],
                      start=True, stop=True).then_inc(att_t_summed, 1)
            keep_warm(WARM[4])
            pe.wait_ge(mixw_in, 16 * NPAIR)
            pe.wait_ge(diag_ready, NPAIR)
            for q in range(OG):
                cols = slice(q % 2 * OSET * TILES, (q % 2 + 1) * OSET * TILES)
                mm = pe.matmul(setup_ps[q // 2][:, cols], mixw_sb[:, q, :, :].rearrange("p b i -> p (b i)"),
                               att_diag[:].rearrange("p o t -> p (o t)"), start=True, stop=True)
                if q % 2 == 1:
                    mm.then_inc(mixw_summed, 1)
                if q == 1:
                    pe.wait_ge(bias_k_in, 16)
                    pe.wait_ge(att_t_ready, 1)
                    pe.matmul(cond_ps[0:BATCH, 0:CHAN], att_t[:], bias_k_sb[:],
                              start=True, stop=True).then_inc(agg_b_summed, 1)
            pe.wait_ge(agg_b_ready, 1)
            for b in range(EARLY):
                mm = pe.matmul(cond_ps[:, 256 + b * CHAN:256 + (b + 1) * CHAN],
                               att_t[:, b:b + 1].to_broadcast([NMIX, P]), bias_k_sb[:], start=True, stop=True)
            mm.then_inc(agg_b_early, 1)

            def mix_chunk(j, s, c):
                h, k = c // BANK_KC, c % BANK_KC
                if k == 0:
                    if c == 0:
                        if isinstance(j, int):
                            pe.wait_ge(x_in[s], 16 * (j // SLOTS + 1))
                        else:
                            pe.wait_ge(x_in[s], (j - s + SLOTS) * (16 // SLOTS))
                    if not is_first(j, 1):
                        pe.wait_ge(u_summed, NBANK * (j - 1) + h + 1)
                mm = pe.matmul(mix_ps[h][:, k, :], x_tile[:, s, c * P:(c + 1) * P], mix_blk[:, j, :],
                               start=True, stop=True)
                if k == BANK_KC - 1:
                    mm.then_inc(mix_done, 1)

            pe.wait_ge(blk_even, OG // 2)
            pe.wait_ge(blk_odd, OG // 2)
            for j in range(GROUP):
                for c in range(KC):
                    mix_chunk(j, j, c)

            def main_chunk(s, c, first_tile, halves=range(NH)):
                lhs = (slice(None), s // GROUP, c, slice((s % GROUP) * P, (s % GROUP + 1) * P))
                if first_tile:
                    pe.wait_ge(w_hi_ready, c + 1)
                    pe.wait_ge(w_lo_ready, c + 1)
                for u_part, w_part in ((u_hi, w_hi), (u_hi, w_lo), (u_lo, w_hi)):
                    for h in halves:
                        pe.matmul(out_ps[s % 2][h][:], u_part[lhs], w_part[:, c, COLS[h]],
                                  start=(c == 0 and u_part is u_hi and w_part is w_hi), stop=False)

            def lora_down(g, parity):
                if not isinstance(g, int) or g > 0:
                    pe.wait_ge(t_summed, g)
                else:
                    pe.wait_ge(a_hi_ready, 1)
                    pe.wait_ge(a_lo_ready, 1)
                pe.wait_ge(u_lo_ready, NBANK * GROUP * (g + 1))
                for c in range(KC):
                    for u_part in (u_hi, u_lo):
                        mm = pe.matmul(t_ps[:], a_parts[:, c, :], u_part[:, parity, c, :],
                                       start=(c == 0 and u_part is u_hi), stop=(c == KC - 1 and u_part is u_lo))
                mm.then_inc(t_done, 1)

            def lora_up(j, s, first_tile, halves=range(NH)):
                if first_tile:
                    pe.wait_ge(b_hi_ready, 1)
                    pe.wait_ge(b_lo_ready, 1)
                if s % GROUP == 0:
                    pe.wait_ge(t_hi_ready, j // GROUP + 1)
                    pe.wait_ge(t_lo_ready, j // GROUP + 1)
                lhs = t_parts[:, s // GROUP, (s % GROUP) * P:(s % GROUP + 1) * P]
                for part in (b_hi, b_lo):
                    for h in halves:
                        mm = pe.matmul(out_ps[s % 2][h][:], lhs, part[:, COLS[h]], start=False, stop=part is b_lo)
                mm.then_inc(tile_done, 1)

            def step(j, s):
                first_tile = is_first(j, 1)
                pe.wait_ge(u_lo_ready, NBANK * (j + 1))
                if not is_first(j, 2):
                    pe.wait_ge(tile_added, j - 1)
                if is_last(j):
                    for h in range(NH):
                        for c in range(KC):
                            main_chunk(s, c, False, [h])
                        lora_up(j, s, False, [h])
                    return
                for c in range(KC):
                    main_chunk(s, c, first_tile)
                    if c == (FIRST_DOWN_CHUNK if first_tile else DOWN_CHUNK) and s % GROUP == 0:
                        lora_down(j // GROUP, s // GROUP)
                    mix = c - KC // 2 if first_tile else c
                    if 0 <= mix < KC // 2 and has_next(j):
                        for m in range(2):
                            mix_chunk(j + GROUP, (s + GROUP) % SLOTS, 2 * mix + m)
                lora_up(j, s, first_tile)

            all_steps(pe, step)


def kernel(**inputs):
    import numpy as np
    import concourse.bacc as bacc
    from concourse.bass_utils import run_bass_kernel_spmd

    def layout(a, shape, axes):
        return np.ascontiguousarray(np.transpose(np.reshape(a, shape), axes))

    i = {name: np.asarray(a) for name, a in inputs.items()}
    arrays = {
        "x": i["x"].reshape(TILES, P, HID),
        "cond_pack": np.concatenate([
            np.transpose(i["cond_128"]), i["L0_cond_W0"], i["L0_cond_W1"], i["L0_cond_W2"],
            i["L0_cond_b0"].reshape(P, 1), i["L0_cond_b1"].reshape(P, 1)], axis=1),
        "b2": i["L0_cond_b2"].reshape(1, NMIX),
        "mixw": layout(i["L0_cond_weight"], (NMIX, OG, OSET, CHAN), (2, 0, 1, 3)).reshape(OSET * NMIX, OG, CHAN),
        "bias_k": i["L0_cond_bias_k"],
        "w_t": layout(i["L0_ffn_weight"], (HID, KC, P), (1, 2, 0)),
        "ffn_bias": i["L0_ffn_bias"].reshape(1, HID),
        "lora_a_t": layout(i["L0_ffn_lora_A"], (LR, KC, P), (2, 1, 0)),
        "lora_b_t": layout(i["L0_ffn_lora_B"], (NLORA, HID, RANK), (0, 2, 1)).reshape(LR, HID),
        "starts": i["L0_ffn_lora_start_indices"].reshape(NLORA + 1, 1),
    }
    arrays = {name: np.ascontiguousarray(a) for name, a in arrays.items()}
    nc = bacc.Bacc("TRN2", target_bir_lowering=False, num_devices=1)
    args = {name: nc.dram_tensor(f"in_{name}", a.shape, mybir.dt.from_np(a.dtype), kind="ExternalInput").ap()
            for name, a in arrays.items()}
    out = nc.dram_tensor("out", (TILES, P, HID), mybir.dt.float32, kind="ExternalOutput").ap()
    adaln_ffn(nc, out=out, **args)
    r = run_bass_kernel_spmd(nc, [{f"in_{name}": a for name, a in arrays.items()}], core_ids=[0])
    return r.results[0]["out"].reshape(BATCH, CHAN, HID)
```

```python
from contextlib import ExitStack

import concourse.bass as bass
from concourse import mybir

BATCH = 64
CHAN = 64
HID = 1024
EMB = 128
NMIX = 8
NLORA = 3
RANK = 16
P = 128
NPAIR = P // CHAN
TILES = BATCH // NPAIR
KC = HID // P
LR = NLORA * RANK
COLS = HID + LR
THIRD = 358
PARTS = [(0, THIRD), (THIRD, 2 * THIRD), (2 * THIRD, COLS)]
ORDER = (2, 0, 1)
NPART = len(ORDER)
W_COLS = [slice(lo, min(hi, HID)) for lo, hi in PARTS]
PIECE_KC = 2
PARTK = KC // PIECE_KC
PIECES = [(h, c) for h in ORDER for c in range(0, KC, PIECE_KC)]
PIECE_SLOTS = 6
WARM = (20, 5, 5, 15)
XT0 = 2
ATT_CHUNK = 6
HALF = 512
NH = HID // HALF
HALVES = [slice(h * HALF, (h + 1) * HALF) for h in range(NH)]
SR = NPAIR * RANK
GROUPS = 3
LOW_T = SR
LOW_B = 2 * SR
MISC = GROUPS * SR
NSUM = 3
BIAS = MISC + NSUM
AGG_ALL, AGG_LOW, AGG_ONE = NPAIR, NPAIR + 1, NPAIR + 2
NAGG = NPAIR + 3
CONST_PARTS = {"batch_of_row": TILES, "batch_of_slot": TILES, "slots": GROUPS * NPAIR, "parity": NPAIR,
               "is_sum": 1, "is_low": 1, "sign": 1, "is_misc": 1}
REP = P // NMIX
OSET = REP // NPAIR
OG = CHAN // OSET
COND_PARTS = {"cond": BATCH, "w0": P, "w1": P, "w2": NMIX, "b0": 1, "b1": 1}


def adaln_ffn(nc, x, x_t, cond_pack, b2, mixw, bias_k, wa, ffn_bias, lora_b, starts, consts, out):
    F32 = mybir.dt.float32
    F32R = mybir.dt.float32r
    I32 = mybir.dt.int32
    ALU = mybir.AluOpType
    ACT = mybir.ActivationFunctionType
    AX_X = mybir.AxisListType.X

    agg_b_dram = nc.dram_tensor("agg_b_scratch", [NAGG, BATCH, CHAN], F32, kind="Internal").ap()

    ctx = ExitStack()
    with ctx:
        def sb(name, shape, dt=F32):
            return ctx.enter_context(nc.sbuf_tensor(name, shape, dt))

        def ps(name, shape):
            return ctx.enter_context(nc.psum_tensor(name, shape, F32))

        def sem(name):
            return ctx.enter_context(nc.semaphore(name))

        wa_hi = sb("wa_hi", [P, KC, COLS], F32R)
        wa_lo = sb("wa_lo", [P, KC, COLS], F32R)
        wa_stage = sb("wa_stage", [P, PIECE_SLOTS, PIECE_KC, THIRD])
        agg_b_all = sb("agg_b_all", [P, BATCH * CHAN])
        wa_two = agg_b_all[:, 0:PIECE_KC * COLS].rearrange("p (q c) -> p q c", q=PIECE_KC)
        wa_sum = sb("wa_sum", [P, COLS])
        x_tile = sb("x_tile", [P, 2, HID])
        xt_stage = sb("xt_stage", [P, 2, KC, P])
        xt_hi = sb("xt_hi", [P, 2, KC, P], F32R)
        xt_lo = sb("xt_lo", [P, 2, KC, P], F32R)
        z_hi = sb("z_hi", [P, 2, HID], F32R)
        z_lo = sb("z_lo", [P, 2, HID], F32R)
        blk_hi = sb("blk_hi", [P, 2, P], F32R)
        blk_lo = sb("blk_lo", [P, 2, P], F32R)
        out_tile = sb("out_tile", [P, 2, HID])
        p_own = sb("p_own", [P, NLORA, RANK])
        p_sum = sb("p_sum", [P, RANK])
        p_sel = sb("p_sel", [P, P])
        t_sum = sb("t_sum", [P, P])
        t_parts = sb("t_parts", [P, P], F32R)
        mix_blk = sb("mix_blk", [P, TILES, P])
        b_all = sb("b_all", [P, NLORA, HID], F32R)
        b_sel = sb("b_sel", [P, 2, HID], F32R)
        ones = sb("ones", [P, P])
        cond_all = sb("cond_all", [P, sum(COND_PARTS.values())])
        cond_part, at = {}, 0
        for name, width in COND_PARTS.items():
            cond_part[name] = cond_all[:, at:at + width]
            at += width
        warm = sb("warm", [P, 1])
        idle = sb("idle", [P, P], mybir.dt.bfloat16)
        b2_sb = sb("b2_sb", [BATCH, NMIX])
        h1 = sb("h1", [P, BATCH])
        h2 = sb("h2", [P, BATCH])
        logits = sb("logits", [BATCH, NMIX])
        top = sb("top", [BATCH, 1])
        neg_top = sb("neg_top", [BATCH, 1])
        expd = sb("expd", [BATCH, NMIX])
        exp_sum = sb("exp_sum", [BATCH, 1])
        exp_inv = sb("exp_inv", [BATCH, 1])
        att_rep = sb("att_rep", [BATCH, REP, NMIX])
        att_t = sb("att_t", [NMIX, BATCH])
        att_diag = sb("att_diag", [P, OSET, TILES])
        diag = sb("diag", [P, REP])
        ident = sb("ident", [BATCH, BATCH])
        mixw_sb = out_tile[:, 0, :].rearrange("p (q b i) -> p q b i", q=OG, b=NPAIR)
        bias_k_sb = sb("bias_k_sb", [NMIX, CHAN])
        agg_b_sb = cond_all[0:BATCH, 0:NAGG * CHAN].rearrange("p (n c) -> p n c", n=NAGG)
        agg_b_hi = sb("agg_b_hi", [BATCH, CHAN], F32R)
        const_all = sb("const_all", [P, sum(CONST_PARTS.values())])
        const, at = {}, 0
        for name, width in CONST_PARTS.items():
            const[name] = const_all[:, at:at + width]
            at += width
        starts_i = sb("starts_i", [P, NLORA + 1], I32)
        starts_f = sb("starts_f", [P, NLORA + 1])
        under = sb("under", [P, TILES])
        over = sb("over", [P, TILES])
        row_masks = sb("row_masks", [P, TILES, NLORA])
        slot_masks = sb("slot_masks", [P, TILES, NLORA + 1])
        slot_now = sb("slot_now", [P, 2, NLORA + 1])
        a_sums = sb("a_sums", [P, NLORA])
        b_stage = [x_tile[:, 0, :], x_tile[:, 1, :], out_tile[:, 1, :]]
        misc_stage = out_tile[:, 0, :]
        a_spread = wa_stage[:, 0, :, :].rearrange("p q c -> p (q c)")[:, 0:NLORA * P].rearrange(
            "p (a r) -> p a r", a=NLORA)

        z_ps = [ps(f"z_ps{h}", [P, HALF]) for h in range(NPART)]
        out_ps = [ps(f"out_ps{h}", [P, HALF]) for h in range(NH)]
        t_ps = ps("t_ps", [P, HALF])
        spare_ps = [ps(f"spare_ps{h}", [P, HALF]) for h in range(NH)]
        cond_ps = t_ps
        setup_ps = [*out_ps, *spare_ps]

        x_in = [sem(f"x_in{s}") for s in range(2)]
        xt_first_in = [sem(f"xt_first_in{i}") for i in range(XT0)]
        xt_in = [sem(f"xt_in{s}") for s in range(2)]
        wa_in = [sem(f"wa_in{n}") for n in range(len(PIECES))]
        cond_in = sem("cond_in")
        b2_in = sem("b2_in")
        mixw_in = sem("mixw_in")
        bias_k_in = sem("bias_k_in")
        starts_in = sem("starts_in")
        b_in = sem("b_in")
        warm_ready = sem("warm_ready")
        warmed = sem("warmed")
        consts_begun = sem("consts_begun")
        idle_ready = sem("idle_ready")
        mixw_cleared = sem("mixw_cleared")
        diag_made = sem("diag_made")
        ident_made = sem("ident_made")
        ones_made = sem("ones_made")
        misc_cleared = sem("misc_cleared")
        const_in = sem("const_in")
        misc_in = sem("misc_in")
        p_sel_cleared = sem("p_sel_cleared")
        agg_one_made = sem("agg_one_made")
        blk_cleared = sem("blk_cleared")
        h1_summed = sem("h1_summed")
        h1_ready = sem("h1_ready")
        h2_summed = sem("h2_summed")
        h2_ready = sem("h2_ready")
        logits_summed = sem("logits_summed")
        logits_ready = sem("logits_ready")
        top_ready = sem("top_ready")
        exp_ready = sem("exp_ready")
        soft = sem("soft")
        att_ready = sem("att_ready")
        att_t_summed = sem("att_t_summed")
        att_t_ready = sem("att_t_ready")
        diag_ready = sem("diag_ready")
        agg_b_summed = sem("agg_b_summed")
        agg_b_ready = sem("agg_b_ready")
        agg_b_hi_ready = sem("agg_b_hi_ready")
        agg_b_low_ready = sem("agg_b_low_ready")
        agg_b_out = sem("agg_b_out")
        agg_b_in = sem("agg_b_in")
        mixw_summed = sem("mixw_summed")
        blk_even = sem("blk_even")
        blk_odd = sem("blk_odd")
        starts_ready = sem("starts_ready")
        bounds_ready = sem("bounds_ready")
        masks_ready = sem("masks_ready")
        a_spread_ready = sem("a_spread_ready")
        a_sums_folded = sem("a_sums_folded")
        p_owned = sem("p_owned")
        p_summed = sem("p_summed")
        slot_now_ready = sem("slot_now_ready")
        b_begun = sem("b_begun")
        b_added = sem("b_added")
        b_sel_ready = sem("b_sel_ready")
        wa_hi_ready = sem("wa_hi_ready")
        wa_lo_ready = sem("wa_lo_ready")
        wa_two_ready = sem("wa_two_ready")
        wa_sum_ready = sem("wa_sum_ready")
        sums_done = sem("sums_done")
        a_sums_ready = sem("a_sums_ready")
        misc_whole = sem("misc_whole")
        misc_signed = sem("misc_signed")
        misc_split = sem("misc_split")
        misc_copied = sem("misc_copied")
        b_hi_ready = sem("b_hi_ready")
        b_lo_ready = sem("b_lo_ready")
        b_lo_last_ready = sem("b_lo_last_ready")
        xt_hi_ready = sem("xt_hi_ready")
        xt_lo_ready = sem("xt_lo_ready")
        blk_hi_ready = sem("blk_hi_ready")
        blk_lo_ready = sem("blk_lo_ready")
        z_done = [sem(f"z_done{k}") for k in range(NPART)]
        z_hi_ready = [sem(f"z_hi_ready{k}") for k in range(NPART)]
        z_lo_ready = [sem(f"z_lo_ready{k}") for k in range(NPART)]
        p_ready = sem("p_ready")
        t_mixed = sem("t_mixed")
        t_summed = sem("t_summed")
        t_hi_ready = sem("t_hi_ready")
        t_lo_ready = sem("t_lo_ready")
        half_done = sem("half_done")
        half_added = sem("half_added")
        stored = [sem(f"stored{s}") for s in range(2)]

        block = ctx.enter_context(nc.Block())

        def all_steps(engine, step):
            for s in range(2):
                step(s, s)
            with engine.Fori(1, TILES // 2 - 1) as turn:
                for s in range(2):
                    step(turn * 2 + s, s)
            for s in range(2):
                step(TILES - 2 + s, s)

        def in_first(j, count):
            return isinstance(j, int) and j < count

        def loads_by(j, s):
            return (j // 2 + 1) * 16 if isinstance(j, int) else (j - s + 2) * 8

        def xt_by(j, s):
            return loads_by(j, s) if s else loads_by(j - 2, s)

        def in_last(j, count):
            return isinstance(j, int) and j >= TILES - count

        @block.sync
        def _(sp):
            def load_xt(j, s):
                sp.dma_start(xt_stage[:, s, :, :], x_t[j]).then_inc(xt_in[s], 16)

            def load_wa(n):
                if n >= PIECE_SLOTS:
                    sp.wait_ge(wa_hi_ready, n - PIECE_SLOTS + 1)
                    sp.wait_ge(wa_lo_ready, n - PIECE_SLOTS + 1)
                    sp.wait_ge(wa_two_ready, n - PIECE_SLOTS + 1)
                (lo, hi), c = PARTS[PIECES[n][0]], PIECES[n][1]
                sp.dma_start(wa_stage[:, n % PIECE_SLOTS, :, 0:hi - lo], wa[:, c:c + PIECE_KC, lo:hi]).then_inc(wa_in[n], 16)

            sp.dma_start(cond_all[:], cond_pack).then_inc(cond_in, 16)
            for i in range(XT0):
                own = slice(i * KC // XT0, (i + 1) * KC // XT0)
                sp.dma_start(xt_stage[:, 0, own, :], x_t[0][:, own, :]).then_inc(xt_first_in[i], 16)
                load_wa(i)
            for n in range(XT0, PARTK):
                load_wa(n)
                if n == XT0:
                    sp.dma_start(b2_sb[:], b2.to_broadcast([BATCH, NMIX])).then_inc(b2_in, 16)
            sp.dma_start(bias_k_sb[:], bias_k).then_inc(bias_k_in, 16)
            sp.dma_start(const_all[:], consts).then_inc(const_in, 16)
            sp.dma_start(starts_i[:], starts.to_broadcast([P, NLORA + 1])).then_inc(starts_in, 16)
            sp.wait_ge(mixw_cleared, 1)
            for b in range(NPAIR):
                sp.dma_start(mixw_sb[b * CHAN:(b + 1) * CHAN, :, b, :], mixw).then_inc(mixw_in, 16)
            for n in range(PARTK, 2 * PARTK):
                load_wa(n)
            load_xt(1, 1)
            for n in range(2 * PARTK, len(PIECES)):
                load_wa(n)
            sp.dma_start(x_tile[0:MISC, :, :], lora_b[:, 0:2, :]).then_inc(b_in, 16)
            sp.dma_start(out_tile[0:MISC, 1, :], lora_b[:, 2, :]).then_inc(b_in, 16)
            sp.wait_ge(xt_lo_ready, XT0)
            load_xt(2, 0)
            sp.wait_ge(agg_one_made, 1)
            sp.wait_ge(agg_b_ready, NPAIR + 1)
            sp.wait_ge(agg_b_low_ready, 1)
            sp.dma_start(agg_b_dram.rearrange("n b c -> b n c"), agg_b_sb[:]).then_inc(agg_b_out, 16)
            sp.wait_ge(misc_cleared, 1)
            for row in (BIAS, BIAS + 1):
                sp.dma_start(misc_stage[row:row + 1, :], ffn_bias).then_inc(misc_in, 16)
            sp.wait_ge(agg_b_out, 16)
            sp.wait_ge(wa_sum_ready, NPART)
            agg_rows = [(row, row + RANK, row // RANK % NPAIR) for row in range(0, MISC, RANK)]
            agg_rows += [(MISC, MISC + 1, AGG_ALL), (MISC + 1, MISC + 2, AGG_LOW), (MISC + 2, BIAS, AGG_ALL),
                         (BIAS, P, AGG_ONE)]
            for lo, hi, n in agg_rows:
                sp.dma_start(agg_b_all[lo:hi, :], agg_b_dram[n:n + 1].rearrange("n b c -> n (b c)")
                             .to_broadcast([hi - lo, BATCH * CHAN])).then_inc(agg_b_in, 16)
            for s in range(2):
                sp.wait_ge(b_hi_ready, 1)
                sp.wait_ge(b_lo_ready, 1)
                sp.dma_start(x_tile[:, s, :], x[s]).then_inc(x_in[s], 16)

            def store(j, s):
                for h in range(NH):
                    if in_last(j, 1) or h == NH - 1:
                        sp.wait_ge(half_added, NH * j + h + 1)
                    if in_last(j, 1):
                        sp.dma_start(out[j][:, HALVES[h]], out_tile[:, s, HALVES[h]]).then_inc(stored[s], 16)
                if not in_last(j, 1):
                    sp.dma_start(out[j], out_tile[:, s, :]).then_inc(stored[s], 16)

            def step(j, s):
                if not in_first(j, 1) and not in_last(j, 2):
                    sp.wait_ge(xt_lo_ready, j + XT0)
                    load_xt(j + 2, s)
                if not in_first(j, 1):
                    store(j - 1, 1 - s)
                    if not in_last(j, 1):
                        sp.dma_start(x_tile[:, 1 - s, :], x[j + 1]).then_inc(x_in[1 - s], 16)

            all_steps(sp, step)
            store(TILES - 1, (TILES - 1) % 2)
            sp.wait_ge(stored[0], 16 * TILES // 2)
            sp.wait_ge(stored[1], 16 * (TILES // 2 - 1 + NH))

        @block.gpsimd
        def _(pool):
            pool.memset(mixw_sb[:], 0.0).then_inc(mixw_cleared, 1)
            pool.wait_ge(mixw_cleared, 1)
            pool.memset(diag[:], 1.0).then_inc(consts_begun, 1)
            pool.wait_ge(consts_begun, 1)
            pool.affine_select(out=diag[:], in_=diag[:], compare_op=ALU.is_ge, fill=0.0, base=0,
                               pattern=[[-NMIX, REP]], channel_multiplier=1).then_inc(consts_begun, 1)
            pool.wait_ge(consts_begun, 2)
            pool.affine_select(out=diag[:], in_=diag[:], compare_op=ALU.is_ge, fill=0.0, base=NMIX - 1,
                               pattern=[[NMIX, REP]], channel_multiplier=-1).then_inc(diag_made, 1)
            pool.memset(ident[:], 0.0).then_inc(consts_begun, 1)
            pool.wait_ge(consts_begun, 3)
            pool.affine_select(out=ident[:], in_=ident[:], compare_op=ALU.not_equal, fill=1.0, base=0,
                               pattern=[[-1, BATCH]], channel_multiplier=1).then_inc(ident_made, 1)
            pool.memset(p_sel[:], 0.0).then_inc(p_sel_cleared, 1)
            pool.memset(ones[:], 1.0).then_inc(ones_made, 1)

            for k, h in enumerate(ORDER):
                lo, hi = PARTS[h]
                pieces = [wa_stage[:, n % PIECE_SLOTS, :, 0:hi - lo] for n in range(k * PARTK, (k + 1) * PARTK)]
                so_far = wa_two[:, :, lo:hi]
                for q in range(1, PARTK):
                    n = k * PARTK + q
                    if q == 1:
                        pool.wait_ge(wa_in[n - 1], 16)
                    else:
                        pool.wait_ge(wa_two_ready, n)
                    pool.wait_ge(wa_in[n], 16)
                    pool.tensor_tensor(so_far, pieces[0] if q == 1 else so_far, pieces[q],
                                       ALU.add).then_inc(wa_two_ready, 2 if q == 1 else 1)
                pool.wait_ge(wa_two_ready, (k + 1) * PARTK)
                pool.tensor_tensor(wa_sum[:, lo:hi], wa_two[:, 0, lo:hi], wa_two[:, 1, lo:hi], ALU.add).then_inc(wa_sum_ready, 1)
                pool.wait_ge(wa_sum_ready, k + 1)
                if k == 0:
                    pool.wait_ge(logits_summed, 1)
                    pool.memset(agg_b_sb[:, AGG_ONE, :], 1.0).then_inc(agg_one_made, 1)
                    pool.wait_ge(agg_one_made, 1)
                if k == 1:
                    pool.wait_ge(mixw_summed, OG // 2)
                    pool.memset(misc_stage[MISC:P, :], 0.0).then_inc(misc_cleared, 1)
                    pool.wait_ge(misc_cleared, 1)

            own = slice(LOW_B, LOW_B + SR)
            pool.wait_ge(b_hi_ready, 2)
            pool.wait_ge(wa_sum_ready, NPART)
            pool.tensor_tensor(b_all[own, 2, :], b_stage[2][own, :], b_all[own, 2, :].bitcast(F32),
                               ALU.subtract).then_inc(b_lo_last_ready, 1)
            pool.wait_ge(b_lo_last_ready, 1)
            pool.wait_ge(xt_hi_ready, 2 + XT0)
            pool.tensor_tensor(xt_lo[:, 0, :, :], xt_stage[:, 0, :, :], xt_hi[:, 0, :, :].bitcast(F32),
                               ALU.subtract).then_inc(xt_lo_ready, 1)

        @block.scalar
        def _(act):
            def xt_high(j, s):
                act.wait_ge(xt_in[s], xt_by(j, s))
                act.activation(xt_hi[:, s, :, :], xt_stage[:, s, :, :], ACT.Copy).then_inc(xt_hi_ready, 1)

            def xt_high_first(i):
                own = slice(i * KC // XT0, (i + 1) * KC // XT0)
                act.wait_ge(xt_first_in[i], 16)
                act.activation(xt_hi[:, 0, own, :], xt_stage[:, 0, own, :], ACT.Copy).then_inc(xt_hi_ready, 1)

            def wa_high(n):
                (lo, hi), c = PARTS[PIECES[n][0]], PIECES[n][1]
                act.wait_ge(wa_in[n], 16)
                act.activation(wa_hi[:, c:c + PIECE_KC, lo:hi], wa_stage[:, n % PIECE_SLOTS, :, 0:hi - lo],
                               ACT.Copy).then_inc(wa_hi_ready, 1)

            def z_high(j, s, k):
                h = ORDER[k]
                act.wait_ge(z_done[k], j + 1)
                cols = W_COLS[h]
                act.activation(z_hi[:, s, cols], z_ps[h][:, 0:cols.stop - cols.start], ACT.Copy).then_inc(z_hi_ready[k], 1)

            def blk_high(j, s):
                if in_first(j, 1):
                    act.wait_ge(blk_even, OG // 2)
                    act.wait_ge(blk_odd, OG // 2)
                act.activation(blk_hi[:, s, :], mix_blk[:, j, :], ACT.Copy).then_inc(blk_hi_ready, 1)

            def t_high(j):
                act.wait_ge(t_summed, j + 1)
                act.activation(t_parts[:], t_sum[:], ACT.Copy).then_inc(t_hi_ready, 1)

            def b_begin(j, s):
                act.wait_ge(slot_now_ready, j + 1)
                act.activation(b_sel[0:MISC, s, :], b_all[0:MISC, 0, :].bitcast(F32), ACT.Copy,
                               scale=slot_now[0:MISC, s, 0:1]).then_inc(b_begun, 1)

            def step(j, s):
                if in_first(j, 1):
                    act.wait_ge(b_in, 32)
                    act.activation(b_all[0:MISC, 0:2, :], x_tile[0:MISC, :, :], ACT.Copy).then_inc(b_hi_ready, 1)
                    act.activation(b_all[0:MISC, 2, :], b_stage[2][0:MISC, :], ACT.Copy).then_inc(b_hi_ready, 1)
                    blk_high(0, 0)
                    return
                z_high(j - 1, 1 - s, 2)
                if not in_last(j, 1):
                    xt_high(j + 1, 1 - s)
                z_high(j, s, 0)
                if in_first(j, 2):
                    act.wait_ge(b_lo_ready, 1)
                    b_begin(0, 0)
                    b_begin(1, 1)
                    act.wait_ge(misc_whole, 1)
                    act.activation(b_sel[MISC:P, 1, :], misc_stage[MISC:P, :], ACT.Copy,
                                   scale=const["sign"][MISC:P, :]).then_inc(misc_signed, 1)
                    z_high(1, 1, 1)
                    blk_high(1, 1)
                    t_high(0)
                    act.wait_ge(misc_split, 1)
                    act.activation(b_sel[MISC:P, 1, :], b_sel[MISC:P, 0, :].bitcast(F32), ACT.Copy).then_inc(misc_copied, 1)
                    act.wait_ge(misc_copied, 1)
                    act.wait_ge(half_done, NH)
                    t_high(1)
                    return
                blk_high(j, s)
                b_begin(j, s)
                z_high(j, s, 1)
                t_high(j)

            act.wait_ge(warm_ready, 1)
            act.activation(warm[:, 0:1], warm[:, 0:1], ACT.Gelu).then_inc(warmed, 1)
            act.wait_ge(h1_summed, 1)
            act.activation(h1[:], cond_ps[:, 0:BATCH], ACT.Gelu, bias=cond_part["b0"]).then_inc(h1_ready, 1)
            xt_high_first(0)
            act.wait_ge(h2_summed, 1)
            act.activation(h2[:], cond_ps[:, BATCH:2 * BATCH], ACT.Gelu, bias=cond_part["b1"]).then_inc(h2_ready, 1)
            wa_high(0)
            xt_high_first(1)
            wa_high(1)
            wa_high(2)
            act.wait_ge(top_ready, 1)
            act.activation(expd[:], logits[:], ACT.Exp, bias=neg_top[:, 0:1],
                           accum_out=exp_sum[:, 0:1]).then_inc(exp_ready, 1)
            for n in range(3, PARTK + 2):
                wa_high(n)
            act.wait_ge(diag_ready, 1)
            act.activation(att_t[:], cond_ps[0:NMIX, 192:192 + BATCH], ACT.Copy).then_inc(att_t_ready, 1)
            for n in range(PARTK + 2, 2 * PARTK):
                wa_high(n)
            z_high(0, 0, 0)
            xt_high(1, 1)
            wa_high(2 * PARTK)
            act.wait_ge(agg_b_summed, 1)
            act.wait_ge(const_in, 16)
            for n in range(NPAIR):
                act.activation(agg_b_sb[:, n, :], cond_ps[0:BATCH, 0:CHAN], ACT.Copy,
                               scale=const["parity"][0:BATCH, n:n + 1]).then_inc(agg_b_ready, 1)
            act.activation(agg_b_sb[:, AGG_ALL, :], cond_ps[0:BATCH, 0:CHAN], ACT.Copy).then_inc(agg_b_ready, 1)
            act.activation(agg_b_hi[:], cond_ps[0:BATCH, 0:CHAN], ACT.Copy).then_inc(agg_b_hi_ready, 1)
            act.wait_ge(blk_cleared, 2)
            for n in range(OG // 2):
                act.wait_ge(mixw_summed, n + 1)
                lo = CHAN + n * 2 * OSET
                act.activation(mix_blk[CHAN:P, :, lo:lo + 2 * OSET].rearrange("p t o -> p o t"),
                               setup_ps[n][CHAN:P, :].rearrange("p (o t) -> p o t", t=TILES),
                               ACT.Copy).then_inc(blk_odd, 1)
                if n < PARTK - 1:
                    wa_high(2 * PARTK + 1 + n)
            z_high(0, 0, 1)
            all_steps(act, step)
            z_high(TILES - 1, (TILES - 1) % 2, 2)

        @block.vector
        def _(dve):
            dve.memset(idle[:], 0.0).then_inc(idle_ready, 1)
            dve.memset(warm[:], 0.0).then_inc(warm_ready, 1)
            dve.memset(mix_blk[0:CHAN, :, CHAN:P], 0.0).then_inc(blk_cleared, 1)
            dve.memset(mix_blk[CHAN:P, :, 0:CHAN], 0.0).then_inc(blk_cleared, 1)

            def xt_low(j, s):
                dve.wait_ge(xt_hi_ready, j + XT0)
                dve.tensor_tensor(xt_lo[:, s, :, :], xt_stage[:, s, :, :], xt_hi[:, s, :, :].bitcast(F32),
                                  ALU.subtract).then_inc(xt_lo_ready, 1)

            def xt_low_first(i):
                own = slice(i * KC // XT0, (i + 1) * KC // XT0)
                dve.wait_ge(xt_hi_ready, i + 1)
                dve.tensor_tensor(xt_lo[:, 0, own, :], xt_stage[:, 0, own, :], xt_hi[:, 0, own, :].bitcast(F32),
                                  ALU.subtract).then_inc(xt_lo_ready, 1)

            def wa_low(n):
                (lo, hi), c = PARTS[PIECES[n][0]], PIECES[n][1]
                dve.wait_ge(wa_hi_ready, n + 1)
                dve.tensor_tensor(wa_lo[:, c:c + PIECE_KC, lo:hi], wa_stage[:, n % PIECE_SLOTS, :, 0:hi - lo],
                                  wa_hi[:, c:c + PIECE_KC, lo:hi].bitcast(F32), ALU.subtract).then_inc(wa_lo_ready, 1)

            def z_low(j, s, k):
                h = ORDER[k]
                cols = W_COLS[h]
                width = cols.stop - cols.start
                if k == 0:
                    dve.wait_ge(z_done[k], j + 1)
                    dve.wait_ge(z_hi_ready[k], j + 1)
                    if in_first(j, 2) and j == 1:
                        dve.wait_ge(t_mixed, 1)
                    p = z_ps[h][:, width:width + LR].rearrange("p (a r) -> p a r", a=NLORA)
                    dve.tensor_tensor(p_own[:], p, row_masks[:, j, :].unsqueeze(2).to_broadcast([P, NLORA, RANK]),
                                      ALU.mult).then_inc(p_owned, 1)
                    dve.wait_ge(p_owned, j + 1)
                    dve.reduce_sum(p_sum[:], p_own[:].rearrange("p a r -> p r a"), AX_X).then_inc(p_summed, 1)
                    dve.wait_ge(p_summed, j + 1)
                    dve.tensor_tensor(p_sel[:, 0:MISC].rearrange("p (g r) -> p g r", r=RANK),
                                      p_sum[:].unsqueeze(1).to_broadcast([P, GROUPS * NPAIR, RANK]),
                                      const["slots"].unsqueeze(2).to_broadcast([P, GROUPS * NPAIR, RANK]),
                                      ALU.mult).then_inc(p_ready, 1)
                dve.wait_ge(z_hi_ready[k], j + 1)
                dve.tensor_tensor(z_lo[:, s, cols], z_ps[h][:, 0:width], z_hi[:, s, cols].bitcast(F32),
                                  ALU.subtract).then_inc(z_lo_ready[k], 1)

            def blk_low(j, s):
                dve.wait_ge(blk_hi_ready, j + 1)
                dve.tensor_tensor(blk_lo[:, s, :], mix_blk[:, j, :], blk_hi[:, s, :].bitcast(F32),
                                  ALU.subtract).then_inc(blk_lo_ready, 1)

            def t_chain(j, s):
                dve.wait_ge(t_mixed, j + 1)
                if in_first(j, 1):
                    dve.wait_ge(agg_b_in, 16 * (GROUPS * NPAIR + NSUM + 1))
                else:
                    dve.wait_ge(t_lo_ready, j)
                dve.scalar_tensor_tensor(out=t_sum[:], in0=agg_b_all[:, bass.ts(j, P)], scalar=slot_now[:, s, NLORA:NLORA + 1],
                                         in1=t_ps[:, 0:P], op0=ALU.mult, op1=ALU.add).then_inc(t_summed, 1)
                dve.wait_ge(t_hi_ready, j + 1)
                dve.tensor_tensor(t_parts[LOW_T:LOW_T + SR, :], t_sum[LOW_T:LOW_T + SR, :],
                                  t_parts[LOW_T:LOW_T + SR, :].bitcast(F32), ALU.subtract).then_inc(t_lo_ready, 1)

            def take_slots(j, s):
                dve.tensor_copy(slot_now[:, s, :], slot_masks[:, j, :]).then_inc(slot_now_ready, 1)

            def b_rest(j, s):
                for a in range(1, NLORA):
                    if a == 1:
                        dve.wait_ge(b_begun, j + 1)
                    else:
                        dve.wait_ge(b_added, j + 1)
                    dve.scalar_tensor_tensor(out=b_sel[0:MISC, s, :], in0=b_all[0:MISC, a, :].bitcast(F32),
                                             scalar=slot_now[0:MISC, s, a:a + 1], in1=b_sel[0:MISC, s, :].bitcast(F32),
                                             op0=ALU.mult, op1=ALU.add).then_inc(b_added if a == 1 else b_sel_ready, 1)

            def make_masks(n):
                batch, masks = ((const["batch_of_row"], row_masks), (const["batch_of_slot"], slot_masks))[n]
                if n == 0:
                    dve.wait_ge(starts_in, 16)
                    dve.wait_ge(const_in, 16)
                    dve.tensor_copy(starts_f[:], starts_i[:]).then_inc(starts_ready, 1)
                    dve.wait_ge(starts_ready, 1)
                else:
                    dve.wait_ge(masks_ready, NLORA)
                dve.tensor_scalar(under[:], batch, starts_f[:, 2:3], None, ALU.is_lt).then_inc(bounds_ready, 1)
                dve.tensor_scalar(over[:], batch, starts_f[:, 2:3], None, ALU.is_ge).then_inc(bounds_ready, 1)
                dve.wait_ge(bounds_ready, 2 * n + 2)
                for a, (start, side, bound) in enumerate(((1, ALU.is_ge, under), (3, ALU.is_lt, over), (3, ALU.is_ge, over))):
                    dve.scalar_tensor_tensor(out=masks[:, :, a], in0=batch, scalar=starts_f[:, start:start + 1],
                                             in1=bound[:], op0=side, op1=ALU.mult).then_inc(masks_ready, 1)

            def spread_a():
                dve.wait_ge(wa_sum_ready, NPART - 1)
                dve.memset(a_spread[:, :, MISC:P], 0.0).then_inc(a_spread_ready, 1)
                for a in range(NLORA):
                    own = wa_sum[:, HID + a * RANK:HID + (a + 1) * RANK]
                    dve.tensor_copy(a_spread[:, a, 0:MISC].rearrange("p (g r) -> p g r", r=RANK),
                                    own.unsqueeze(1).to_broadcast([P, GROUPS * NPAIR, RANK])).then_inc(a_spread_ready, 1)

            def fold_a_sums():
                dve.wait_ge(masks_ready, 2 * NLORA)
                dve.wait_ge(sums_done, 1)
                dve.tensor_copy(a_sums[:], spare_ps[1][:, 0:NLORA]).then_inc(a_sums_ready, 1)
                dve.wait_ge(a_sums_ready, 1)
                into = slot_masks[:, :, NLORA]
                dve.tensor_scalar(into, slot_masks[:, :, 0], a_sums[:, 0:1], const["is_misc"], ALU.mult, ALU.add).then_inc(a_sums_folded, 1)
                for a in range(1, NLORA):
                    dve.wait_ge(a_sums_folded, a)
                    dve.scalar_tensor_tensor(out=into, in0=slot_masks[:, :, a], scalar=a_sums[:, a:a + 1], in1=into,
                                             op0=ALU.mult, op1=ALU.add).then_inc(a_sums_folded, 1)
                dve.wait_ge(a_sums_folded, NLORA)

            def add_x(j, s):
                dve.wait_ge(x_in[s], loads_by(j, s))
                if not in_first(j, 2):
                    dve.wait_ge(stored[s], (j - s) * 8)
                for h in range(NH):
                    dve.wait_ge(half_done, NH * j + h + 1)
                    dve.tensor_tensor(out_tile[:, s, HALVES[h]], out_ps[h][:], x_tile[:, s, HALVES[h]],
                                      ALU.add).then_inc(half_added, 1)

            def step(j, s):
                if in_first(j, 1):
                    spread_a()
                    make_masks(1)
                    own = slice(LOW_B, LOW_B + SR)
                    dve.wait_ge(b_hi_ready, 1)
                    dve.tensor_tensor(b_all[own, 0:2, :], x_tile[own, :, :], b_all[own, 0:2, :].bitcast(F32),
                                      ALU.subtract).then_inc(b_lo_ready, 1)
                    blk_low(0, 0)
                    return
                if in_first(j, 2):
                    fold_a_sums()
                    take_slots(0, 0)
                    take_slots(1, 1)
                    z_low(0, 0, 2)
                    dve.wait_ge(sums_done, NH + 1)
                    dve.wait_ge(misc_in, 32)
                    for h, bank in enumerate((spare_ps[0], out_ps[1])):
                        last = dve.scalar_tensor_tensor(out=misc_stage[MISC:P, HALVES[h]], in0=bank[MISC:P, :],
                                                        scalar=const["is_sum"][MISC:P, :], in1=misc_stage[MISC:P, HALVES[h]],
                                                        op0=ALU.mult, op1=ALU.add)
                    last.then_inc(misc_whole, 1)
                    z_low(1, 1, 0)
                    dve.wait_ge(b_lo_last_ready, 1)
                    b_rest(0, 0)
                    t_chain(0, 0)
                    dve.wait_ge(misc_signed, 1)
                    dve.scalar_tensor_tensor(out=b_sel[MISC:P, 0, :], in0=misc_stage[MISC:P, :], scalar=const["is_low"][MISC:P, :],
                                             in1=b_sel[MISC:P, 1, :].bitcast(F32), op0=ALU.mult, op1=ALU.add).then_inc(misc_split, 1)
                    z_low(1, 1, 1)
                    blk_low(1, 1)
                    b_rest(1, 1)
                    t_chain(1, 1)
                    add_x(0, 0)
                    dve.wait_ge(xt_lo_ready, 2 + XT0)
                    return
                z_low(j - 1, 1 - s, 2)
                if not in_last(j, 1):
                    xt_low(j + 1, 1 - s)
                z_low(j, s, 0)
                take_slots(j, s)
                blk_low(j, s)
                add_x(j - 1, 1 - s)
                b_rest(j, s)
                z_low(j, s, 1)
                t_chain(j, s)

            xt_low_first(0)
            wa_low(0)
            xt_low_first(1)
            wa_low(1)
            dve.wait_ge(logits_summed, 1)
            dve.wait_ge(b2_in, 16)
            dve.tensor_tensor(logits[:], cond_ps[0:BATCH, 128:128 + NMIX], b2_sb[:], ALU.add).then_inc(logits_ready, 1)
            dve.wait_ge(logits_ready, 1)
            dve.reduce_max(top[:], logits[:], AX_X).then_inc(soft, 1)
            dve.wait_ge(soft, 1)
            dve.tensor_scalar(neg_top[:], top[:], -1.0, None, ALU.mult).then_inc(top_ready, 1)
            wa_low(2)
            dve.wait_ge(exp_ready, 1)
            dve.reciprocal(exp_inv[:], exp_sum[:]).then_inc(soft, 1)
            dve.wait_ge(soft, 2)
            dve.tensor_scalar(att_rep[:], expd[:].unsqueeze(1).to_broadcast([BATCH, REP, NMIX]),
                              exp_inv[:, 0:1], None, ALU.mult).then_inc(att_ready, 1)
            wa_low(3)
            dve.wait_ge(att_t_summed, 1)
            dve.wait_ge(diag_made, 1)
            for b in range(NPAIR):
                rows, groups = slice(b * CHAN, (b + 1) * CHAN), slice(b * OSET, (b + 1) * OSET)
                own = cond_ps[rows, 192:192 + BATCH].rearrange("p (t b) -> p b t", b=NPAIR)[:, b, :]
                dve.tensor_tensor(att_diag[rows, :, :], own.unsqueeze(1).to_broadcast([CHAN, OSET, TILES]),
                                  diag[rows, groups].unsqueeze(2).to_broadcast([CHAN, OSET, TILES]),
                                  ALU.mult).then_inc(diag_ready, 1)
            for n in range(PARTK, 2 * PARTK):
                wa_low(n)
                if n == PARTK + 1:
                    make_masks(0)
            dve.wait_ge(masks_ready, NLORA)
            z_low(0, 0, 0)
            xt_low(1, 1)
            wa_low(2 * PARTK)
            dve.wait_ge(agg_b_hi_ready, 1)
            dve.tensor_tensor(agg_b_sb[:, AGG_LOW, :], cond_ps[0:BATCH, 0:CHAN], agg_b_hi[:].bitcast(F32),
                              ALU.subtract).then_inc(agg_b_low_ready, 1)
            for n in range(OG // 2):
                dve.wait_ge(mixw_summed, n + 1)
                lo = n * 2 * OSET
                dve.tensor_copy(mix_blk[0:CHAN, :, lo:lo + 2 * OSET].rearrange("p t o -> p o t"),
                                setup_ps[n][0:CHAN, :].rearrange("p (o t) -> p o t", t=TILES)).then_inc(blk_even, 1)
                if n < PARTK - 1:
                    wa_low(2 * PARTK + 1 + n)
            z_low(0, 0, 1)

            all_steps(dve, step)
            z_low(TILES - 1, (TILES - 1) % 2, 2)
            add_x(TILES - 1, (TILES - 1) % 2)

        @block.tensor
        def _(pe):
            def keep_warm(n):
                for _ in range(n):
                    pe.matmul(setup_ps[-1][:, 0:P], idle[:], idle[:], start=True, stop=True)

            pe.wait_ge(idle_ready, 1)
            keep_warm(WARM[0])
            pe.wait_ge(cond_in, 16)
            pe.matmul(cond_ps[:, 0:BATCH], cond_part["w0"], cond_part["cond"], start=True, stop=True).then_inc(h1_summed, 1)
            keep_warm(WARM[1])
            pe.wait_ge(h1_ready, 1)
            pe.matmul(cond_ps[:, BATCH:2 * BATCH], cond_part["w1"], h1[:], start=True, stop=True).then_inc(h2_summed, 1)
            keep_warm(WARM[2])
            pe.wait_ge(h2_ready, 1)
            pe.matmul(cond_ps[0:BATCH, 128:128 + NMIX], h2[:], cond_part["w2"], start=True, stop=True).then_inc(logits_summed, 1)
            keep_warm(WARM[3])

            def main_part(j, s, k, chunks=range(KC)):
                h = ORDER[k]
                lo, hi = PARTS[h]
                if not in_first(j, 1):
                    pe.wait_ge(z_lo_ready[k], j)
                    if k == 0:
                        pe.wait_ge(xt_lo_ready, j + XT0)
                for c in chunks:
                    if in_first(j, 1) and k == 0 and c % (KC // XT0) == 0:
                        pe.wait_ge(xt_lo_ready, c // (KC // XT0) + 1)
                    if in_first(j, 1) and c % PIECE_KC == 0:
                        n = PIECES.index((h, c))
                        pe.wait_ge(wa_hi_ready, n + 1)
                        pe.wait_ge(wa_lo_ready, n + 1)
                    for i, (x_part, w_part) in enumerate(((xt_hi, wa_hi), (xt_hi, wa_lo), (xt_lo, wa_hi))):
                        mm = pe.matmul(z_ps[h][:, 0:hi - lo], x_part[:, s, c, :], w_part[:, c, lo:hi],
                                       start=(c == 0 and i == 0), stop=(c == KC - 1 and i == 2))
                if chunks[-1] == KC - 1:
                    mm.then_inc(z_done[k], 1)

            def mix_p(j):
                pe.wait_ge(p_ready, j + 1)
                if in_first(j, 1):
                    pe.wait_ge(p_sel_cleared, 1)
                    pe.wait_ge(agg_b_low_ready, 1)
                    pe.wait_ge(agg_b_hi_ready, 1)
                    pe.wait_ge(blk_even, OG // 2)
                    pe.wait_ge(blk_odd, OG // 2)
                else:
                    pe.wait_ge(t_summed, j)
                pe.matmul(t_ps[:, 0:P], p_sel[:], mix_blk[:, j, :], start=True, stop=True).then_inc(t_mixed, 1)

            def finish(j, s):
                def mix_z(h):
                    for i, (blk, z) in enumerate(((blk_hi, z_hi), (blk_hi, z_lo), (blk_lo, z_hi))):
                        pe.matmul(out_ps[h][:], blk[:, s, :], z[:, s, HALVES[h]], start=i == 0, stop=False)

                pe.wait_ge(blk_lo_ready, j + 1)
                for k in range(NPART):
                    pe.wait_ge(z_lo_ready[k], j + 1)
                if in_first(j, 1):
                    pe.wait_ge(misc_whole, 1)
                    for h in range(NH):
                        mix_z(h)
                for h in range(NH):
                    if not in_first(j, 1):
                        pe.wait_ge(half_added, NH * (j - 1) + h + 1)
                        mix_z(h)
                    if h == 0:
                        if in_first(j, 1):
                            pe.wait_ge(misc_split, 1)
                        pe.wait_ge(b_sel_ready, j + 1)
                        pe.wait_ge(t_hi_ready, j + 1)
                        pe.wait_ge(t_lo_ready, j + 1)
                    mm = pe.matmul(out_ps[h][:], t_parts[:], b_sel[:, s, HALVES[h]], start=False, stop=True)
                    mm.then_inc(half_done, 1)

            def finish_last(j, s):
                for h in range(NH):
                    pe.wait_ge(half_added, NH * (j - 1) + h + 1)
                    if h == 0:
                        pe.wait_ge(b_sel_ready, j + 1)
                        pe.wait_ge(t_hi_ready, j + 1)
                        pe.wait_ge(t_lo_ready, j + 1)
                    pe.matmul(out_ps[h][:], t_parts[:], b_sel[:, s, HALVES[h]], start=True, stop=False)
                pe.wait_ge(blk_lo_ready, j + 1)
                for k in range(NPART):
                    pe.wait_ge(z_lo_ready[k], j + 1)
                    for h in range(NH):
                        lo = max(W_COLS[ORDER[k]].start, HALVES[h].start)
                        hi = min(W_COLS[ORDER[k]].stop, HALVES[h].stop)
                        if lo >= hi:
                            continue
                        for i, (blk, z) in enumerate(((blk_hi, z_hi), (blk_hi, z_lo), (blk_lo, z_hi))):
                            mm = pe.matmul(out_ps[h][:, lo - HALVES[h].start:hi - HALVES[h].start], blk[:, s, :],
                                           z[:, s, lo:hi], start=False, stop=k == NPART - 1 and i == 2)
                        if k == NPART - 1:
                            mm.then_inc(half_done, 1)

            def attention():
                pe.wait_ge(ident_made, 1)
                pe.wait_ge(att_ready, 1)
                pe.matmul(cond_ps[:, 192:192 + BATCH], att_rep[:].rearrange("b g k -> b (g k)"), ident[:],
                          start=True, stop=True).then_inc(att_t_summed, 1)

            def mixing():
                pe.wait_ge(mixw_in, 16 * NPAIR)
                pe.wait_ge(diag_ready, NPAIR)
                for q in range(OG):
                    cols = slice(q % 2 * OSET * TILES, (q % 2 + 1) * OSET * TILES)
                    mm = pe.matmul(setup_ps[q // 2][:, cols], mixw_sb[:, q, :, :].rearrange("p b i -> p (b i)"),
                                   att_diag[:].rearrange("p o t -> p (o t)"), start=True, stop=True)
                    if q % 2 == 1:
                        mm.then_inc(mixw_summed, 1)
                    if q == 1:
                        pe.wait_ge(bias_k_in, 16)
                        pe.wait_ge(att_t_ready, 1)
                        pe.matmul(cond_ps[0:BATCH, 0:CHAN], att_t[:], bias_k_sb[:],
                                  start=True, stop=True).then_inc(agg_b_summed, 1)

            def weight_sums():
                pe.wait_ge(ones_made, 1)
                pe.wait_ge(a_spread_ready, NLORA + 1)
                for a in range(NLORA):
                    mm = pe.matmul(spare_ps[1][:, a:a + 1], a_spread[:, a, :], ones[:, 0:1], start=True, stop=True)
                mm.then_inc(sums_done, 1)
                pe.wait_ge(wa_sum_ready, NPART)
                for h, bank in enumerate((spare_ps[0], out_ps[1])):
                    pe.matmul(bank[:], ones[:], wa_sum[:, HALVES[h]], start=True, stop=True).then_inc(sums_done, 1)

            def step(j, s):
                if in_first(j, 1):
                    main_part(0, 0, 0, range(ATT_CHUNK))
                    attention()
                    main_part(0, 0, 0, range(ATT_CHUNK, KC))
                    mixing()
                    main_part(0, 0, 1)
                    main_part(1, 1, 0)
                    main_part(0, 0, 2)
                    mix_p(0)
                    return
                if in_first(j, 2):
                    weight_sums()
                    main_part(1, 1, 1)
                    main_part(1, 1, 2)
                    finish(0, 0)
                    mix_p(1)
                    return
                main_part(j, s, 0)
                finish(j - 1, 1 - s)
                main_part(j, s, 1)
                mix_p(j)
                main_part(j, s, 2)

            all_steps(pe, step)
            finish_last(TILES - 1, (TILES - 1) % 2)


def kernel(**inputs):
    import numpy as np
    import concourse.bacc as bacc
    from concourse.bass_utils import run_bass_kernel_spmd

    def layout(a, shape, axes):
        return np.ascontiguousarray(np.transpose(np.reshape(a, shape), axes))

    row = np.arange(P).reshape(P, 1)
    slot_of_row, slot_of_rank = row // CHAN, row // RANK % NPAIR
    shape_consts = {
        "batch_of_row": NPAIR * np.arange(TILES).reshape(1, TILES) + slot_of_row,
        "batch_of_slot": NPAIR * np.arange(TILES).reshape(1, TILES) + slot_of_rank,
        "slots": np.arange(GROUPS * NPAIR).reshape(1, -1) % NPAIR == slot_of_row,
        "parity": np.arange(NPAIR).reshape(1, NPAIR) == row % NPAIR,
        "is_sum": (row >= MISC) & (row < BIAS),
        "is_low": (row == BIAS - 1) | (row == BIAS + 1),
        "sign": 1 - 2 * ((row == BIAS - 1) | (row == BIAS + 1)),
        "is_misc": row >= MISC,
    }
    i = {name: np.asarray(a) for name, a in inputs.items()}
    arrays = {
        "x": i["x"].reshape(TILES, P, HID),
        "x_t": layout(i["x"], (TILES, P, KC, P), (0, 3, 2, 1)),
        "cond_pack": np.concatenate([
            np.transpose(i["cond_128"]), i["L0_cond_W0"], i["L0_cond_W1"], i["L0_cond_W2"],
            i["L0_cond_b0"].reshape(P, 1), i["L0_cond_b1"].reshape(P, 1)], axis=1),
        "b2": i["L0_cond_b2"].reshape(1, NMIX),
        "mixw": layout(i["L0_cond_weight"], (NMIX, OG, OSET, CHAN), (2, 0, 1, 3)).reshape(OSET * NMIX, OG, CHAN),
        "bias_k": i["L0_cond_bias_k"],
        "wa": layout(np.concatenate([i["L0_ffn_weight"], i["L0_ffn_lora_A"].reshape(LR, HID)]), (COLS, KC, P), (2, 1, 0)),
        "ffn_bias": i["L0_ffn_bias"].reshape(1, HID),
        "lora_b": np.tile(layout(i["L0_ffn_lora_B"], (NLORA, HID, RANK), (2, 0, 1)), (GROUPS * NPAIR, 1, 1)),
        "starts": i["L0_ffn_lora_start_indices"].reshape(1, NLORA + 1),
        "consts": np.concatenate([shape_consts[name] for name in CONST_PARTS], axis=1).astype(np.float32),
    }
    arrays = {name: np.ascontiguousarray(a) for name, a in arrays.items()}
    nc = bacc.Bacc("TRN2", target_bir_lowering=False, num_devices=1)
    args = {name: nc.dram_tensor(f"in_{name}", a.shape, mybir.dt.from_np(a.dtype), kind="ExternalInput").ap()
            for name, a in arrays.items()}
    out = nc.dram_tensor("out", (TILES, P, HID), mybir.dt.float32, kind="ExternalOutput").ap()
    adaln_ffn(nc, out=out, **args)
    r = run_bass_kernel_spmd(nc, [{f"in_{name}": a for name, a in arrays.items()}], core_ids=[0])
    return r.results[0]["out"].reshape(BATCH, CHAN, HID)
```
